# Optimizing a Trainium2 kernel written in Bass

```python
import numpy as np
import jax
import jax.numpy as jnp

def _softmax(x, axis=-1):
    return jax.nn.softmax(x, axis=axis)

def _gelu(x):
    return jax.nn.gelu(x, approximate=True)

def _silu(x):
    return jax.nn.silu(x)

def _sigmoid(x):
    return jax.nn.sigmoid(x)

def _layernorm(x, axis=-1, eps=1e-05):
    m = jnp.mean(x, axis=axis, keepdims=True)
    v = jnp.var(x, axis=axis, keepdims=True)
    return (x - m) / jnp.sqrt(v + eps)

def _scatter_add(tgt, idx, src, axis=0):
    return tgt.at[idx].add(src)

def _segment_sum(src, seg, n):
    return jax.ops.segment_sum(src, seg, n)
kernel_name = 'mk_sandwich_d1_jaxref_r8_c48d06'

def setup_inputs(seed: int=0):
    np.random.seed(seed)
    _w = jnp.asarray

    def _L0_attn_setup():
        import jax, jax.numpy as jnp
        import numpy as np
        DEPTH, DIM, DFF, VOCAB = (4, 64, 256, 512)
        EPS = 1e-05

        def layernorm(x, w, b):
            mu = jnp.mean(x, axis=-1, keepdims=True)
            var = jnp.mean((x - mu) ** 2, axis=-1, keepdims=True)
            return (x - mu) * jax.lax.rsqrt(var + EPS) * w + b

        def sconv(x, phazor_c, last_conv_c):
            B, L, D = x.shape
            r = jnp.abs(phazor_c)
            p = jnp.tanh(r) * jnp.exp(1j * jnp.angle(phazor_c))
            prog = p[None, :] ** jnp.arange(L, dtype=jnp.float32)[:, None]
            filt_fft = jnp.fft.fft(prog, n=2 * L, axis=0)
            x_fft = jnp.fft.fft(x.astype(jnp.complex64), n=2 * L, axis=1)
            conv = jnp.fft.ifft(filt_fft[None] * x_fft, axis=1)[:, :L]
            conv = conv + last_conv_c[None, None, :] * prog[None] * p[None, None, :]
            return conv.real.astype(x.dtype)

        def _forward(x, Win, bin, ln1_w, ln1_b, phz_re, phz_im, lc_re, lc_im, sc_lin, ln2_w, ln2_b, W1, b1, W2, b2, lnl_w, lnl_b, Wout, bout):
            h = jnp.einsum('blv,dv->bld', x, Win) + bin

            def body(h, p):
                l1w, l1b, pr, pi, lr, li, scl, l2w, l2b, w1, b1_, w2, b2_ = p
                y = jax.nn.silu(layernorm(h, l1w, l1b))
                y = sconv(y, pr + 1j * pi, lr + 1j * li)
                h = h + y * scl
                y = layernorm(h, l2w, l2b)
                y = jax.nn.silu(jnp.einsum('bld,fd->blf', y, w1) + b1_)
                y = jnp.einsum('blf,df->bld', y, w2) + b2_
                return (h + y, None)
            xs = (ln1_w, ln1_b, phz_re, phz_im, lc_re, lc_im, sc_lin, ln2_w, ln2_b, W1, b1, W2, b2)
            h, _ = jax.lax.scan(body, h, xs)
            h = layernorm(h, lnl_w, lnl_b)
            return jnp.einsum('bld,vd->blv', h, Wout) + bout
        key = jax.random.key(seed)
        ks = jax.random.split(key, 20)
        f32 = jnp.float32
        inp = {}
        inp['x'] = jax.random.normal(ks[0], (2, 512, VOCAB), dtype=f32)
        inp['Win'] = jax.random.normal(ks[1], (DIM, VOCAB), dtype=f32) * VOCAB ** (-0.5)
        inp['bin'] = jnp.zeros((DIM,), f32)
        inp['ln1_w'] = jnp.ones((DEPTH, DIM), f32)
        inp['ln1_b'] = jnp.zeros((DEPTH, DIM), f32)
        ang = 2 * np.pi * jnp.arange(DIM, dtype=f32) / DIM
        mag = jnp.abs(jax.random.normal(ks[2], (DEPTH, DIM), dtype=f32))
        inp['phz_re'] = mag * jnp.cos(ang)[None]
        inp['phz_im'] = mag * jnp.sin(ang)[None]
        inp['lc_re'] = jax.random.normal(ks[3], (DEPTH, DIM), dtype=f32)
        inp['lc_im'] = jax.random.normal(ks[4], (DEPTH, DIM), dtype=f32)
        inp['sc_lin'] = jnp.ones((DEPTH, DIM), f32)
        inp['ln2_w'] = jnp.ones((DEPTH, DIM), f32)
        inp['ln2_b'] = jnp.zeros((DEPTH, DIM), f32)
        inp['W1'] = jax.random.normal(ks[5], (DEPTH, DFF, DIM), dtype=f32) * DIM ** (-0.5)
        inp['b1'] = jnp.zeros((DEPTH, DFF), f32)
        inp['W2'] = jax.random.normal(ks[6], (DEPTH, DIM, DFF), dtype=f32) * DFF ** (-0.5)
        inp['b2'] = jnp.zeros((DEPTH, DIM), f32)
        inp['lnl_w'] = jnp.ones((DIM,), f32)
        inp['lnl_b'] = jnp.zeros((DIM,), f32)
        inp['Wout'] = jax.random.normal(ks[7], (VOCAB, DIM), dtype=f32) * DIM ** (-0.5)
        inp['bout'] = jnp.zeros((VOCAB,), f32)
        return inp
    _L0_attn_in = _L0_attn_setup()

    def _L0_ffn_setup():
        import jax, jax.numpy as jnp
        import numpy as np
        HID, BOT, RDIM, NSLOT, K, VB = (512, 64, 48, 128, 8, 32)
        TAU_LOW, TAU_HIGH, EARLY_EXIT = (0.5, 2.0, 0.05)

        def _uncertainty(h, Wu1, bu1, Wu2, bu2):
            var = jnp.var(h, axis=-1)
            log_var = jnp.log1p(var)
            norm_var = log_var / (jnp.mean(log_var) + 1e-06)
            learned = (jax.nn.gelu(h @ Wu1.T + bu1) @ Wu2.T + bu2)[..., 0]
            return jnp.clip(norm_var * 0.5 + jax.nn.sigmoid(learned) * 2.5, 0.0, 5.0)
        key = jax.random.key(seed)
        ks = jax.random.split(key, 12)
        B, S = (2, 256)
        return {'hidden_states': jax.random.normal(ks[0], (B, S, HID), dtype=jnp.float32), 'Wq': jax.random.normal(ks[1], (BOT, HID), dtype=jnp.float32) / np.sqrt(HID), 'Wr': jax.random.normal(ks[2], (RDIM, BOT), dtype=jnp.float32) / np.sqrt(BOT), 'aux_keys': jax.random.normal(ks[3], (NSLOT, BOT), dtype=jnp.float32) * 0.01, 'aux_values': jax.random.normal(ks[4], (NSLOT, HID), dtype=jnp.float32) * 0.02, 'Wvd': jax.random.normal(ks[5], (VB, HID), dtype=jnp.float32) * 0.1 / np.sqrt(HID), 'Wvu': jax.random.normal(ks[6], (HID, VB), dtype=jnp.float32) * 0.1 / np.sqrt(VB), 'Wu1': jax.random.normal(ks[7], (HID // 4, HID), dtype=jnp.float32) / np.sqrt(HID), 'bu1': jnp.zeros((HID // 4,), dtype=jnp.float32), 'Wu2': jax.random.normal(ks[8], (1, HID // 4), dtype=jnp.float32) * 0.01, 'bu2': jnp.zeros((1,), dtype=jnp.float32), 'gate_w1': jnp.float32(0.5), 'gate_bias': jnp.float32(-1.0), 'log_rel': jnp.zeros((NSLOT,), dtype=jnp.float32)}
    _L0_ffn_in = _L0_ffn_setup()
    _d = {'L0_attn_x': _L0_attn_in['x'], 'L0_attn_Win': _L0_attn_in['Win'], 'L0_attn_bin': _L0_attn_in['bin'], 'L0_attn_ln1_w': _L0_attn_in['ln1_w'], 'L0_attn_ln1_b': _L0_attn_in['ln1_b'], 'L0_attn_phz_re': _L0_attn_in['phz_re'], 'L0_attn_phz_im': _L0_attn_in['phz_im'], 'L0_attn_lc_re': _L0_attn_in['lc_re'], 'L0_attn_lc_im': _L0_attn_in['lc_im'], 'L0_attn_sc_lin': _L0_attn_in['sc_lin'], 'L0_attn_ln2_w': _L0_attn_in['ln2_w'], 'L0_attn_ln2_b': _L0_attn_in['ln2_b'], 'L0_attn_W1': _L0_attn_in['W1'], 'L0_attn_b1': _L0_attn_in['b1'], 'L0_attn_W2': _L0_attn_in['W2'], 'L0_attn_b2': _L0_attn_in['b2'], 'L0_attn_lnl_w': _L0_attn_in['lnl_w'], 'L0_attn_lnl_b': _L0_attn_in['lnl_b'], 'L0_attn_Wout': _L0_attn_in['Wout'], 'L0_attn_bout': _L0_attn_in['bout'], 'L0_ffn_Wq': _L0_ffn_in['Wq'], 'L0_ffn_Wr': _L0_ffn_in['Wr'], 'L0_ffn_aux_keys': _L0_ffn_in['aux_keys'], 'L0_ffn_aux_values': _L0_ffn_in['aux_values'], 'L0_ffn_Wvd': _L0_ffn_in['Wvd'], 'L0_ffn_Wvu': _L0_ffn_in['Wvu'], 'L0_ffn_Wu1': _L0_ffn_in['Wu1'], 'L0_ffn_bu1': _L0_ffn_in['bu1'], 'L0_ffn_Wu2': _L0_ffn_in['Wu2'], 'L0_ffn_bu2': _L0_ffn_in['bu2'], 'L0_ffn_gate_w1': _L0_ffn_in['gate_w1'], 'L0_ffn_gate_bias': _L0_ffn_in['gate_bias'], 'L0_ffn_log_rel': _L0_ffn_in['log_rel']}
    _x0 = _d['L0_attn_x']
    _d['L0_attn_x'] = jax.random.normal(jax.random.fold_in(jax.random.key(seed), 1), (8, 256, 512), dtype=_x0.dtype)
    del _x0
    return _d

def reference(L0_attn_x, L0_attn_Win, L0_attn_bin, L0_attn_ln1_w, L0_attn_ln1_b, L0_attn_phz_re, L0_attn_phz_im, L0_attn_lc_re, L0_attn_lc_im, L0_attn_sc_lin, L0_attn_ln2_w, L0_attn_ln2_b, L0_attn_W1, L0_attn_b1, L0_attn_W2, L0_attn_b2, L0_attn_lnl_w, L0_attn_lnl_b, L0_attn_Wout, L0_attn_bout, L0_ffn_Wq, L0_ffn_Wr, L0_ffn_aux_keys, L0_ffn_aux_values, L0_ffn_Wvd, L0_ffn_Wvu, L0_ffn_Wu1, L0_ffn_bu1, L0_ffn_Wu2, L0_ffn_bu2, L0_ffn_gate_w1, L0_ffn_gate_bias, L0_ffn_log_rel):

    def _L0_attn_ref(x, Win, bin, ln1_w, ln1_b, phz_re, phz_im, lc_re, lc_im, sc_lin, ln2_w, ln2_b, W1, b1, W2, b2, lnl_w, lnl_b, Wout, bout):
        import jax, jax.numpy as jnp
        import numpy as np
        DEPTH, DIM, DFF, VOCAB = (4, 64, 256, 512)
        EPS = 1e-05

        def layernorm(x, w, b):
            mu = jnp.mean(x, axis=-1, keepdims=True)
            var = jnp.mean((x - mu) ** 2, axis=-1, keepdims=True)
            return (x - mu) * jax.lax.rsqrt(var + EPS) * w + b

        def sconv(x, phazor_c, last_conv_c):
            B, L, D = x.shape
            r = jnp.abs(phazor_c)
            p = jnp.tanh(r) * jnp.exp(1j * jnp.angle(phazor_c))
            prog = p[None, :] ** jnp.arange(L, dtype=jnp.float32)[:, None]
            filt_fft = jnp.fft.fft(prog, n=2 * L, axis=0)
            x_fft = jnp.fft.fft(x.astype(jnp.complex64), n=2 * L, axis=1)
            conv = jnp.fft.ifft(filt_fft[None] * x_fft, axis=1)[:, :L]
            conv = conv + last_conv_c[None, None, :] * prog[None] * p[None, None, :]
            return conv.real.astype(x.dtype)

        def _forward(x, Win, bin, ln1_w, ln1_b, phz_re, phz_im, lc_re, lc_im, sc_lin, ln2_w, ln2_b, W1, b1, W2, b2, lnl_w, lnl_b, Wout, bout):
            h = jnp.einsum('blv,dv->bld', x, Win) + bin

            def body(h, p):
                l1w, l1b, pr, pi, lr, li, scl, l2w, l2b, w1, b1_, w2, b2_ = p
                y = jax.nn.silu(layernorm(h, l1w, l1b))
                y = sconv(y, pr + 1j * pi, lr + 1j * li)
                h = h + y * scl
                y = layernorm(h, l2w, l2b)
                y = jax.nn.silu(jnp.einsum('bld,fd->blf', y, w1) + b1_)
                y = jnp.einsum('blf,df->bld', y, w2) + b2_
                return (h + y, None)
            xs = (ln1_w, ln1_b, phz_re, phz_im, lc_re, lc_im, sc_lin, ln2_w, ln2_b, W1, b1, W2, b2)
            h, _ = jax.lax.scan(body, h, xs)
            h = layernorm(h, lnl_w, lnl_b)
            return jnp.einsum('bld,vd->blv', h, Wout) + bout
        return _forward(x, Win, bin, ln1_w, ln1_b, phz_re, phz_im, lc_re, lc_im, sc_lin, ln2_w, ln2_b, W1, b1, W2, b2, lnl_w, lnl_b, Wout, bout)

    def _L0_ffn_ref(hidden_states, Wq, Wr, aux_keys, aux_values, Wvd, Wvu, Wu1, bu1, Wu2, bu2, gate_w1, gate_bias, log_rel):
        import jax, jax.numpy as jnp
        import numpy as np
        HID, BOT, RDIM, NSLOT, K, VB = (512, 64, 48, 128, 8, 32)
        TAU_LOW, TAU_HIGH, EARLY_EXIT = (0.5, 2.0, 0.05)

        def _uncertainty(h, Wu1, bu1, Wu2, bu2):
            var = jnp.var(h, axis=-1)
            log_var = jnp.log1p(var)
            norm_var = log_var / (jnp.mean(log_var) + 1e-06)
            learned = (jax.nn.gelu(h @ Wu1.T + bu1) @ Wu2.T + bu2)[..., 0]
            return jnp.clip(norm_var * 0.5 + jax.nn.sigmoid(learned) * 2.5, 0.0, 5.0)
        query = hidden_states @ Wq.T
        rq = query @ Wr.T
        rk = aux_keys @ Wr.T
        router_scores = jnp.einsum('bsr,nr->bsn', rq, rk) / np.sqrt(RDIM) + log_rel
        top_scores, top_idx = jax.lax.top_k(router_scores, K)
        sel_keys = aux_keys[top_idx]
        attn = jnp.einsum('bsd,bskd->bsk', query, sel_keys) / np.sqrt(BOT) + log_rel[top_idx]
        w = jax.nn.softmax(attn, axis=-1)
        sel_vals = aux_values[top_idx]
        aux_out = jnp.einsum('bsk,bskh->bsh', w, sel_vals)
        aux_out = aux_out @ Wvd.T @ Wvu.T
        u = _uncertainty(hidden_states, Wu1, bu1, Wu2, bu2)
        u_norm = jnp.clip((u - TAU_LOW) / (TAU_HIGH - TAU_LOW), 0.0, 1.0)
        gate = jax.nn.sigmoid(gate_w1 * u_norm + gate_bias)
        gate = jnp.where(gate < EARLY_EXIT, 0.0, gate)
        return hidden_states + gate[..., None] * aux_out
    x = L0_attn_x
    x = x + _layernorm(_L0_attn_ref(_layernorm(x, axis=-1), L0_attn_Win, L0_attn_bin, L0_attn_ln1_w, L0_attn_ln1_b, L0_attn_phz_re, L0_attn_phz_im, L0_attn_lc_re, L0_attn_lc_im, L0_attn_sc_lin, L0_attn_ln2_w, L0_attn_ln2_b, L0_attn_W1, L0_attn_b1, L0_attn_W2, L0_attn_b2, L0_attn_lnl_w, L0_attn_lnl_b, L0_attn_Wout, L0_attn_bout), axis=-1)
    x = x + _layernorm(_L0_ffn_ref(_layernorm(x, axis=-1), L0_ffn_Wq, L0_ffn_Wr, L0_ffn_aux_keys, L0_ffn_aux_values, L0_ffn_Wvd, L0_ffn_Wvu, L0_ffn_Wu1, L0_ffn_bu1, L0_ffn_Wu2, L0_ffn_bu2, L0_ffn_gate_w1, L0_ffn_gate_bias, L0_ffn_log_rel), axis=-1)
    return x

_drawn_inputs = setup_inputs


def setup_inputs(seed=0):
    import zlib

    import numpy as np

    out = dict(_drawn_inputs(seed))
    spreads = {'L0_attn_bin': (0.0, 0.1),
     'L0_attn_ln1_w': (1.0, 0.2),
     'L0_attn_ln1_b': (0.0, 0.1),
     'L0_attn_sc_lin': (1.0, 0.2),
     'L0_attn_ln2_w': (1.0, 0.2),
     'L0_attn_ln2_b': (0.0, 0.1),
     'L0_attn_b1': (0.0, 0.322),
     'L0_attn_b2': (0.0, 0.1),
     'L0_attn_lnl_w': (1.0, 0.2),
     'L0_attn_lnl_b': (0.0, 0.1),
     'L0_attn_bout': (0.0, 0.1),
     'L0_ffn_bu1': (0.0, 2.0),
     'L0_ffn_log_rel': (0.0, 2.0)}
    factors = {'L0_ffn_Wq': 64.0,
     'L0_ffn_Wr': 64.0,
     'L0_ffn_aux_keys': 64.0,
     'L0_ffn_aux_values': 64.0,
     'L0_ffn_Wvd': 64.0,
     'L0_ffn_Wvu': 64.0,
     'L0_ffn_Wu1': 64.0,
     'L0_ffn_Wu2': 64.0}
    for name, (base, spread) in spreads.items():
        noise = np.random.default_rng([zlib.crc32(name.encode()), seed]).standard_normal(out[name].shape)
        drawn = base * np.exp(spread * noise) if base else spread * noise
        out[name] = jnp.asarray(drawn.astype(out[name].dtype))
    for name, factor in factors.items():
        out[name] = (out[name] * factor).astype(out[name].dtype)
    return out
```

```python
from contextlib import ExitStack

import numpy as np
from concourse import mybir

ALU = mybir.AluOpType
ACT = mybir.ActivationFunctionType
AX = mybir.AxisListType
F32 = mybir.dt.float32

P = 128
DEPTH, DIM, DFF, VOCAB = 4, 64, 256, 512
SEQS, LEN = 8, 256
TOK = SEQS * LEN
TILES = TOK // P
GT = 4
GROUPS = TILES // GT
GW = GT * P
SG = GW // LEN
SL = LEN + 1
UC = SG * SL
HC = GT * DIM
VC = VOCAB // P
BOT, RDIM, NSLOT, VB, UH = 64, 48, 128, 32, 128
EPS = 1e-5
TINY = 1e-30
BIG = 1e30
LOWEST = -3e38
UNITS = DEPTH * GROUPS
SW = 2 * NSLOT + UH

CH = {n: i * DEPTH for i, n in enumerate(["re", "im", "lre", "lim", "scl", "w", "b"])}
CHN = 7 * DEPTH
LATE = {}
_at = 0
for _n, _k in (("vals", VC * NSLOT), ("wvd", VC * VB), ("wu2", UH), ("bu2", 1), ("gw", 1), ("gb", 1)):
    LATE[_n] = (_at, _at + _k)
    _at += _k
LATEN = _at
C64 = {}
_at = 0
for _n, _k in (("w2", DEPTH), ("b2", DEPTH), ("lw", 1), ("lb", 1), ("w1t", DEPTH * DFF), ("wout", VOCAB),
               ("wrt", RDIM), ("keys", NSLOT), ("wq", VOCAB)):
    C64[_n] = (_at, _at + _k)
    _at += _k
C64N = _at
TA0, MX0, LW0, LB0, DC0 = 0, SL, SL + DIM, SL + DIM + 1, SL + DIM + 2
NCV = DC0 + UC
NFF = 2 * DIM + 2
PAIRS = TILES // 2


def build(nc, x, xT, win, binb, ch, c64, w2t, b1, b2b, late, wu1, wr, wvu, boutr, srow, out):
    with ExitStack() as ctx:
        def sb(name, shape):
            return ctx.enter_context(nc.sbuf_tensor(name, shape, F32))

        def sem(name):
            return ctx.enter_context(nc.semaphore(name))

        X = sb("X", [P, TILES, VOCAB])
        XT = sb("XT", [P, GROUPS, VC, GW])
        XN = XT[:, :, :, :].rearrange("p g c t -> p (g c) t")
        H = sb("H", [P, GROUPS, HC])
        HB = sb("HB", [P, GROUPS, HC])
        ident = sb("ident", [P, P])
        ones = sb("ones", [P, P])
        nhalf = sb("nhalf", [P, GT])
        epst = sb("epst", [P, GT])
        centre = sb("centre", [P, DIM])
        sgn = sb("sgn", [P, 1])
        winr = sb("winr", [P, VC, DIM])
        binr = sb("binr", [P, DIM])
        chp = sb("chp", [P, CHN])
        c6 = sb("c6", [DIM, C64N])
        w2r = sb("w2r", [P, DEPTH * 2, DIM])
        b1r = sb("b1r", [P, DEPTH * 2])
        b2r = sb("b2r", [P, DEPTH, DIM])
        lt = sb("lt", [P, LATEN])
        wr_s = sb("wr_s", [RDIM, BOT])
        wvu_s = sb("wvu_s", [VB, VOCAB])
        winc = sb("winc", [P, VC, DIM])
        wcc = sb("wcc", [P, VC, DIM])
        binc = sb("binc", [P, DIM])
        cvst = sb("cvst", [P, DEPTH, NCV])
        ffst = sb("ffst", [P, DEPTH, NFF])
        w1st = sb("w1st", [P, DEPTH, DFF])
        b2st = sb("b2st", [P, DEPTH, DIM])
        T2 = sb("T2", [P, DEPTH, LEN // 2])
        tmpA = sb("tmpA", [P, DEPTH, LEN // 2])
        tmpB = sb("tmpB", [P, DEPTH, LEN // 2])
        CS = sb("CS", [P, 9, 2, DEPTH])
        pol = sb("pol", [P, 12, DEPTH])
        WO = sb("WO", [P, VOCAB])
        WOR = sb("WOR", [DIM + 1, VOCAB])
        KB = sb("KB", [BOT, 2 * NSLOT])
        SW_ = sb("SW_", [P, VC, SW])
        SWR = sb("SWR", [1, SW])
        V2 = sb("V2", [NSLOT, VOCAB])
        V2R = sb("V2R", [NSLOT, VOCAB])
        lbp = sb("lbp", [DIM, DIM + 1])
        rkT = sb("rkT", [RDIM, NSLOT])
        vpT = sb("vpT", [VB, NSLOT])
        sm = sb("sm", [P, 64])
        SQ = sb("SQ", [P, GROUPS, HC])
        SS = sb("SS", [P, GROUPS, GT])
        VE = sb("VE", [P, GROUPS, GT])
        RS = sb("RS", [P, GROUPS, GT])
        Z = sb("Z", [P, GROUPS, 2 * HC])
        Y = sb("Y", [P, GROUPS, UC])
        U = sb("U", [P, GROUPS, UC])
        V = sb("V", [P, GROUPS, UC])
        Z2 = sb("Z2", [P, GROUPS, GW])
        HD = sb("HD", [P, 2, 2, GW])
        BN = sb("BN", [P, TILES, 6])
        MV = sb("MV", [P, TILES, 2])
        VX, RX, OSQ, OV, OR, V1X, R1X, LRN, NMX, ES, GS, RES, ZQ, ZV, ZR = (
            sb(n, [P, TILES]) for n in ("VX", "RX", "OSQ", "OV", "OR", "V1X", "R1X", "LRN", "NMX", "ES", "GS",
                                        "RES", "ZQ", "ZV", "ZR"))
        MV1 = sb("MV1", [P, TILES, 2])
        M8 = sb("M8", [P, 2, 8])
        GA = sb("GA", [P, 24, TILES])
        gsum = sb("gsum", [P, 4])
        REP, OFS = tmpA, tmpB
        AM = cvst[:, :, :].rearrange("p l n -> p (l n)")[:, 0:TILES * NSLOT].rearrange("p (t n) -> p t n", t=TILES)
        XNT = Y
        GE = V[:, 0, 0:4 * UH].rearrange("p (t n) -> p t n", t=4)
        GJ = V[:, 1, 0:2 * UH].rearrange("p (t n) -> p t n", t=2)
        JK = V[:, 2:4, 0:GW]
        E_ = U[:, 0:2, 0:2 * NSLOT]
        ET = U[:, 2:4, 0:2 * P]

        bank = [ctx.enter_context(nc.psum_tensor(f"bank{i}", [P, 512], F32)) for i in range(8)]
        T1B, T2B = bank[0], bank[1]
        FB = bank[2:6]
        D1B, D2B = bank[6], bank[7]
        OB = bank[2:4]
        SBK = bank[4:8]

        s_ch, s_win, s_c64, s_w2, s_late, s_rows = (sem(n) for n in (
            "s_ch", "s_win", "s_c64", "s_w2", "s_late", "s_rows"))
        s_xt = [sem(f"s_xt{g}") for g in range(GROUPS)]
        s_x = [sem(f"s_x{g}") for g in range(GROUPS)]
        pool_const = sem("pool_const")
        pool_step = sem("pool_step")
        polar_q, polar_inv = sem("polar_q"), sem("polar_inv")
        polar_r, decay = sem("polar_r"), sem("decay")
        dve_step = sem("dve_step")
        win_ready, win_mean, win_done = sem("win_ready"), sem("win_mean"), sem("win_done")
        b1_mm, b1_read, bo_mm, rk_mm, g_mm, vp_mm, v2_mm, sw_mm, sw_read = (sem(n) for n in (
            "b1_mm", "b1_read", "bo_mm", "rk_mm", "g_mm", "vp_mm", "v2_mm", "sw_mm", "sw_read"))
        rk_sb, vp_sb, kb_sb, act_step = sem("rk_sb"), sem("vp_sb"), sem("kb_sb"), sem("act_step")
        wo_row, sums_ready, sums_scaled = sem("wo_row"), sem("sums_ready"), sem("sums_scaled")
        cv_store, table_done, ff_done, b2_done = sem("cv_store"), sem("table_done"), sem("ff_done"), sem("b2_done")
        w1_store = sem("w1_store")
        late_ready = sem("late_ready")
        x_stats, x_ve, x_rstd, bn_done, h0_mm, h0_done = (sem(n) for n in (
            "x_stats", "x_ve", "x_rstd", "bn_done", "h0_mm", "h0_done"))
        sq1, ss1, ve1, rs1, z1, t1, y1, u1, v1, w1, d1, a1 = (sem(n + "1") for n in (
            "squared", "sumsq", "vareps", "rstd", "z", "turned", "y", "u", "v", "w", "delta", "h_added"))
        sq2, ss2, ve2, rs2, z2, t2, e2, f2, g2, d2, a2 = (sem(n + "2") for n in (
            "squared", "sumsq", "vareps", "rstd", "z", "turned", "z_out", "hidden", "silu", "delta", "h_added"))
        hb = sem("hb")
        o_mm, o_sq, o_ve, o_rstd, x1_done = (sem(n) for n in ("o_mm", "o_sq", "o_ve", "o_rstd", "x1_done"))
        bn1_done, mv1_done, v1_ve, r1_ready, xn_done, xtr, xtr_read = (sem(n) for n in (
            "bn1_done", "mv1_done", "v1_ve", "r1_ready", "xn_done", "xtr", "xtr_read"))
        s_mm, gelu_done, lrn_done, top_found, top_marked, top_ofs, sc_read, am_max = (sem(n) for n in (
            "s_mm", "gelu_done", "lrn_done", "top_found", "top_marked", "top_ofs", "sc_read", "am_max"))
        ga_step, ln_in, ln_out, gsum_in, gsum_mm, sig_in, sig_out, gate_in, gate_out = (sem(n) for n in (
            "ga_step", "ln_in", "ln_out", "gsum_in", "gsum_mm", "sig_in", "sig_out", "gate_in", "gate_out"))
        e_ready, e_tr, et_ready, aux_mm, es_inv, gs_ready, zz_ready, z_sq, z_ve, z_rstd, out_ready, s_out = (
            sem(n) for n in ("e_ready", "e_tr", "et_ready", "aux_mm", "es_inv", "gs_ready", "zz_ready", "z_sq",
                             "z_ve", "z_rstd", "out_ready", "s_out"))

        def c6c(name, a=0, b=None):
            lo, hi = C64[name]
            return c6[:, lo + a:(hi if b is None else lo + b)]

        def ltc(name):
            return lt[:, LATE[name][0]:LATE[name][1]]

        def chc(name):
            return chp[:, CH[name]:CH[name] + DEPTH]

        def rows(ap, n, w):
            return ap.unsqueeze(2).to_broadcast([ap.shape[0], n, w])

        def by_tile(ap):
            return ap.rearrange("p (j d) -> p j d", j=GT)

        def by_seq(ap):
            return ap.rearrange("p (s l) -> p s l", s=SG)

        x_v = x.rearrange("(g j p) v -> g p j v", p=P, j=GT)
        out_v = out.rearrange("(k j p) v -> k p j v", p=P, j=2)
        table = cvst[:, :, TA0 + 1:TA0 + SL]
        STEPS = UNITS + GROUPS
        EARLY = 2
        LAG = 2

        block = ctx.enter_context(nc.Block())

        @block.sync
        def _(sp):
            sp.dma_start(chp[:, :], ch).then_inc(s_ch, 16)
            sp.dma_start(winr[:, :, :], win).then_inc(s_win, 16)
            sp.dma_start(binr[:, :], binb).then_inc(s_win, 16)
            for g in range(GROUPS):
                sp.dma_start(X[:, g * GT:(g + 1) * GT, :], x_v[g]).then_inc(s_x[g], 16)
                sp.dma_start(XT[:, g, :, :], xT[:, g]).then_inc(s_xt[g], 16)
                if g == 0:
                    sp.dma_start(c6[:, :], c64).then_inc(s_c64, 16)
                    sp.dma_start(w2r[:, :, :], w2t).then_inc(s_w2, 16)
                    sp.dma_start(b1r[:, :], b1).then_inc(s_w2, 16)
                    sp.dma_start(b2r[:, :, :], b2b).then_inc(s_w2, 16)
                if g == 1:
                    sp.dma_start(lt[:, :], late).then_inc(s_late, 16)
                    sp.dma_start(wr_s[:, :], wr).then_inc(s_late, 16)
                    sp.dma_start(wvu_s[:, :], wvu).then_inc(s_late, 16)
                    sp.dma_start(WOR[DIM:DIM + 1, :], boutr).then_inc(s_rows, 16)
                    sp.dma_start(SWR[:, :], srow).then_inc(s_rows, 16)
                    sp.dma_start(SW_[:, :, 2 * NSLOT:SW], wu1).then_inc(s_rows, 16)
            for k in range(PAIRS):
                sp.wait_ge(out_ready, 2 * k + 2)
                sp.dma_start(out_v[k], X[:, 2 * k:2 * k + 2, :]).then_inc(s_out, 16)
            sp.wait_ge(s_out, 16 * PAIRS)

        @block.gpsimd
        def _(pool):
            pool.memset(ident[:, :], 0.0).then_inc(pool_step, 1)
            pool.memset(centre[:, :], -1.0 / DIM).then_inc(pool_step, 1)
            pool.memset(nhalf[:, :], -0.5).then_inc(pool_step, 1)
            pool.memset(ones[:, :], 1.0).then_inc(pool_step, 1)
            pool.memset(epst[:, :], EPS).then_inc(pool_step, 1)
            pool.wait_ge(pool_step, 2)
            pool.affine_select(out=ident[:, :], in_=ident[:, :], compare_op=ALU.not_equal, fill=1.0, base=0,
                               pattern=[[-1, P]], channel_multiplier=1).then_inc(pool_step, 1)
            pool.affine_select(out=centre[:, :], in_=centre[:, :], compare_op=ALU.not_equal, fill=1.0 - 1.0 / DIM,
                               base=0, pattern=[[-1, DIM]], channel_multiplier=1).then_inc(pool_step, 1)
            pool.wait_ge(pool_step, 7)
            pool.affine_select(out=centre[:, :], in_=centre[:, :], compare_op=ALU.not_equal, fill=1.0 - 1.0 / DIM,
                               base=-DIM, pattern=[[-1, DIM]], channel_multiplier=1).then_inc(pool_step, 1)
            pool.wait_ge(pool_step, 8)
            pool.memset(lbp[:, :], 0.0).then_inc(pool_const, 1)
            pool.wait_ge(polar_q, 1)
            pool.tensor_tensor(pol[:, 7, :], pol[:, 6, :], nhalf[:, 0:DEPTH], ALU.pow).then_inc(polar_inv, 1)

            def input_rstd(g):
                a, b = g * GT, (g + 1) * GT
                pool.wait_ge(x_stats, g + 1)
                pool.tensor_tensor(VX[:, a:b], MV[:, a:b, 1], epst[:, :], ALU.add).then_inc(x_ve, 1)
                pool.wait_ge(x_ve, g + 1)
                pool.tensor_tensor(RX[:, a:b], VX[:, a:b], nhalf[:, :], ALU.pow).then_inc(x_rstd, 1)

            def norm(u, summed, eps_added, done):
                g = u % GROUPS
                pool.wait_ge(summed, u + 1)
                pool.tensor_tensor(VE[:, g, :], SS[:, g, :], epst[:, :], ALU.add).then_inc(eps_added, 1)
                pool.wait_ge(eps_added, u + 1)
                pool.tensor_tensor(RS[:, g, :], VE[:, g, :], nhalf[:, :], ALU.pow).then_inc(done, 1)

            def add_b2(u):
                g, L = u % GROUPS, u // GROUPS
                pool.wait_ge(a1, u + 1)
                if u == 0:
                    pool.wait_ge(b2_done, 1)
                pool.tensor_tensor(by_tile(HB[:, g, :]), by_tile(H[:, g, :]),
                                   b2st[:, L, :].unsqueeze(1).to_broadcast([P, GT, DIM]), ALU.add).then_inc(hb, 1)

            def step(s):
                norm(s, ss1, ve1, rs1)
                if s + 1 < GROUPS:
                    input_rstd(s + 1)
                if 0 <= s - 1 < UNITS:
                    add_b2(s - 1)
                    norm(s - 1, ss2, ve2, rs2)

            def pair_rstd(k, done, src, mid, mid_done, dst, dst_done):
                a, b = 2 * k, 2 * k + 2
                pool.wait_ge(done, b)
                pool.tensor_tensor(mid[:, a:b], src[:, a:b], epst[:, 0:2], ALU.add).then_inc(mid_done, 1)
                pool.wait_ge(mid_done, k + 1)
                pool.tensor_tensor(dst[:, a:b], mid[:, a:b], nhalf[:, 0:2], ALU.pow).then_inc(dst_done, 1)

            input_rstd(0)
            for s in range(STEPS - EARLY):
                step(s)
                if s == 2:
                    pool.wait_ge(sums_ready, 3)
                    pool.tensor_scalar(sm[:, 2:4], sm[:, 0:2], -1.0 / VOCAB, 0.0, ALU.mult, ALU.add) \
                        .then_inc(sums_scaled, 1)
            for k in range(PAIRS + 1):
                if k < EARLY:
                    step(STEPS - EARLY + k)
                if k >= 1:
                    pair_rstd(k - 1, mv1_done, MV1[:, :, 1], V1X, v1_ve, R1X, r1_ready)
                if k < PAIRS:
                    pair_rstd(k, o_sq, OSQ, OV, o_ve, OR, o_rstd)
            for k in range(PAIRS):
                pair_rstd(k, z_sq, ZQ, ZV, z_ve, ZR, z_rstd)

        @block.scalar
        def _(act):
            act.wait_ge(pool_const, 1)
            act.wait_ge(s_ch, 16)
            for L in range(DEPTH):
                act.activation(cvst[:, L, MX0:MX0 + DIM], centre[:, :], ACT.Copy,
                               scale=chp[:, CH["scl"] + L:CH["scl"] + L + 1])
            act.activation(cvst[:, :, LW0], chc("w"), ACT.Copy)
            act.activation(cvst[:, :, LB0], chc("b"), ACT.Copy).then_inc(cv_store, 1)
            act.wait_ge(polar_r, 1)
            act.activation(pol[:, 9, :], pol[:, 8, :], ACT.Tanh).then_inc(decay, 1)
            act.wait_ge(decay, 1)
            for L in range(DEPTH):
                for q in range(SG):
                    lo = DC0 + q * SL + 1
                    last = act.activation(cvst[:, L, lo:lo + LEN], ones[:, :].unsqueeze(1).to_broadcast([P, 2, P]),
                                          ACT.Copy, scale=pol[:, 9, L:L + 1])
            last.then_inc(cv_store, 1)
            act.wait_ge(cv_store, 2)
            act.wait_ge(s_c64, 16)
            for L in range(DEPTH):
                act.activation(w1st[0:DIM, L, :], c6c("w1t", L * DFF, (L + 1) * DFF), ACT.Copy,
                               scale=c6c("w2", L, L + 1)).then_inc(w1_store, 1)
            act.activation(lbp[:, DIM:DIM + 1], c6c("lb"), ACT.Copy).then_inc(act_step, 1)

            def setup_late():
                act.wait_ge(b1_mm, 1)
                act.activation(sm[:, 8:16], FB[0][:, 0:8], ACT.Copy).then_inc(b1_read, 1)
                act.activation(WOR[0:DIM, :], c6c("wout"), ACT.Copy, scale=c6c("lw"),
                               accum_out=sm[0:DIM, 0:1]).then_inc(sums_ready, 1)
                act.wait_ge(rk_mm, 1)
                act.activation(rkT[:, :], FB[2][0:RDIM, 0:NSLOT], ACT.Copy).then_inc(rk_sb, 1)
                act.wait_ge(vp_mm, 1)
                act.activation(vpT[:, :], FB[3][0:VB, 0:NSLOT], ACT.Copy).then_inc(vp_sb, 1)
                act.activation(KB[:, NSLOT:2 * NSLOT], c6c("keys"), ACT.Copy, scale=float(BOT) ** -0.5)
                act.wait_ge(g_mm, 1)
                act.activation(KB[:, 0:NSLOT], FB[0][0:BOT, 0:NSLOT], ACT.Copy, scale=float(RDIM) ** -0.5) \
                    .then_inc(kb_sb, 1)
                act.wait_ge(v2_mm, 1)
                act.activation(V2R[:, :], FB[2][:, :], ACT.Copy, accum_out=sm[:, 1:2]).then_inc(sums_ready, 1)
                for c in range(0, VC, 2):
                    act.wait_ge(sw_mm, c // 2 + 1)
                    act.activation(SW_[:, c:c + 2, 0:2 * NSLOT],
                                   FB[c // 2 + 2 if c == 2 else 0][:, :].rearrange("p (c n) -> p c n", c=2),
                                   ACT.Copy).then_inc(sw_read, 1)

            def setup_last():
                act.wait_ge(sums_scaled, 1)
                act.activation(V2[:, :], V2R[:, :], ACT.Identity, bias=sm[:, 3:4])
                act.activation(WO[0:DIM + 1, :], WOR[:, :], ACT.Identity, bias=sm[0:DIM + 1, 2:3]).then_inc(late_ready, 1)

            def square(u, ready, done):
                g = u % GROUPS
                if ready is not None:
                    act.wait_ge(*ready)
                act.activation(SQ[:, g, :], H[:, g, :], ACT.Square, scale=float(DIM) ** -0.5).then_inc(done, 1)

            def silu1(u):
                g, L = u % GROUPS, u // GROUPS
                act.wait_ge(t1, u + 1)
                act.activation(by_seq(Y[:, g, :])[:, :, 1:SL], by_seq(T1B[:, :]), ACT.Silu,
                               bias=cvst[:, L, LB0:LB0 + 1], scale=cvst[:, L, LW0:LW0 + 1]).then_inc(y1, 1)

            def last_z(u):
                act.wait_ge(t1, u + 1)
                act.activation(Z2[0:DIM, u % GROUPS, :], T1B[0:DIM, :], ACT.Copy).then_inc(y1, 1)

            def z_out(u):
                act.wait_ge(t2, u + 1)
                act.activation(Z2[0:DIM, u % GROUPS, :], T2B[0:DIM, :], ACT.Copy).then_inc(e2, 1)

            def silu2(u, a):
                g, L = u % GROUPS, u // GROUPS
                act.wait_ge(f2, 2 * u + a + 1)
                if u == 0:
                    act.wait_ge(ff_done, 1)
                act.activation(HD[:, u % 2, a, :], FB[(2 * u + a) % 4][:, :], ACT.Silu,
                               bias=ffst[:, L, 2 * DIM + a:2 * DIM + a + 1]).then_inc(g2, 1)

            def step(s):
                if s < STEPS:
                    square(s, (h0_done, s + 1) if s < GROUPS else (a2, s - GROUPS + 1), sq1)
                ffn = 0 <= s - 2 < UNITS
                if ffn:
                    z_out(s - 2)
                if 0 <= s - 1 < UNITS:
                    square(s - 1, (a1, s), sq2)
                if ffn:
                    silu2(s - 2, 0)
                if s < UNITS:
                    silu1(s)
                else:
                    last_z(s)
                if ffn:
                    silu2(s - 2, 1)

            def out_square(t):
                act.wait_ge(o_mm, t + 1)
                if t >= 2:
                    act.wait_ge(o_sq, t - 1)
                act.activation(JK[:, t % 2, :], OB[t % 2][:, :], ACT.Square, scale=float(VOCAB) ** -0.5,
                               accum_out=OSQ[:, t:t + 1]).then_inc(o_sq, 1)

            def xn_out(t):
                act.wait_ge(xtr, t + 1)
                act.activation(XNT[:, t % 4, 0:GW], bank[t % 2][:, :], ACT.Copy).then_inc(xtr_read, 1)

            def gelu(t):
                act.wait_ge(s_mm, t + 1)
                if t >= 4:
                    act.wait_ge(lrn_done, t - 3)
                act.activation(GE[:, t % 4, :], SBK[t % 4][:, 2 * NSLOT:SW], ACT.Gelu_apprx_tanh) \
                    .then_inc(gelu_done, 1)

            for s in range(STEPS - EARLY):
                if s == 1:
                    setup_late()
                if s == 3:
                    setup_last()
                step(s)
            for k in range(PAIRS + LAG):
                if k < EARLY:
                    step(STEPS - EARLY + k)
                back = 2 * (k - LAG)
                if back >= 0:
                    xn_out(back)
                    xn_out(back + 1)
                for j in range(2):
                    if k < PAIRS:
                        out_square(2 * k + j)
                    if back >= 0:
                        gelu(back + j)

            act.wait_ge(ln_in, 1)
            act.activation(GA[:, 3, :], GA[:, 2, :], ACT.Ln).then_inc(ln_out, 1)

            def exps(k):
                if k == 0:
                    act.wait_ge(am_max, GROUPS)
                if k >= 2:
                    act.wait_ge(e_tr, k - 1)
                for j in range(2):
                    t = 2 * k + j
                    act.activation(E_[:, k % 2, j * NSLOT:(j + 1) * NSLOT], AM[:, t, :], ACT.Exp,
                                   bias=NMX[:, t:t + 1], accum_out=ES[:, t:t + 1]).then_inc(e_ready, 1)

            def e_out(k):
                act.wait_ge(e_tr, k + 1)
                act.activation(ET[:, k % 2, :], bank[k % 2][:, 0:2 * P], ACT.Copy).then_inc(et_ready, 1)

            def z_square(t):
                act.wait_ge(zz_ready, t + 1)
                if t >= 2:
                    act.wait_ge(z_sq, t - 1)
                act.activation(JK[:, t % 2, :], XN[:, t, :], ACT.Square, scale=float(VOCAB) ** -0.5,
                               accum_out=ZQ[:, t:t + 1]).then_inc(z_sq, 1)

            exps(0)
            act.wait_ge(sig_in, 1)
            act.activation(GA[:, 9, :], GA[:, 8, :], ACT.Exp, scale=-1.0).then_inc(sig_out, 1)
            exps(1)
            e_out(0)
            act.wait_ge(gate_in, 1)
            act.activation(GA[:, 16, :], GA[:, 15, :], ACT.Exp, scale=-1.0).then_inc(gate_out, 1)
            for k in range(2, PAIRS + 3):
                if k - 1 < PAIRS:
                    e_out(k - 1)
                if 0 <= k - 3 < PAIRS:
                    z_square(2 * (k - 3))
                if k < PAIRS:
                    exps(k)
                if 0 <= k - 3 < PAIRS:
                    z_square(2 * (k - 3) + 1)

        @block.vector
        def _(dve):
            chain = [0]

            def link(ins):
                chain[0] += 1
                ins.then_inc(dve_step, 1)
                dve.wait_ge(dve_step, chain[0])

            for q in range(SG):
                dve.memset(Y[:, :, q * SL], 1.0)
                dve.memset(cvst[:, :, DC0 + q * SL], 0.0)
            dve.memset(w1st[DIM:P, :, :], 0.0)
            dve.memset(WO[DIM:P, :], 0.0)
            link(dve.memset(Z2[DIM:P, :, :], 0.0))
            dve.memset(Z2[DIM:DIM + 1, :, :], 1.0)
            dve.memset(sm[DIM:P, 0:1], 0.0)
            dve.memset(sgn[0:DIM, :], 1.0)
            dve.memset(sgn[DIM:P, :], -1.0)
            dve.memset(table[0:DIM, :, 0], 1.0)
            dve.memset(table[DIM:P, :, 0], 0.0)
            dve.memset(T2[0:DIM, :, 0], 0.0)
            link(dve.memset(T2[DIM:P, :, 0], 1.0))
            dve.wait_ge(s_ch, 16)
            dve.tensor_scalar(pol[:, 0, :], chc("re"), -1.0, None, ALU.mult)
            link(dve.tensor_scalar(pol[:, 1, :], chc("im"), -1.0, None, ALU.mult))
            dve.tensor_tensor(pol[:, 2, :], pol[:, 0, :], chc("re"), ALU.max)
            link(dve.tensor_tensor(pol[:, 3, :], pol[:, 1, :], chc("im"), ALU.max))
            link(dve.tensor_tensor(pol[:, 4, :], pol[:, 2, :], pol[:, 3, :], ALU.max))
            link(dve.tensor_scalar(pol[:, 5, :], pol[:, 4, :], TINY, None, ALU.max))
            link(dve.reciprocal(pol[:, 10, :], pol[:, 5, :]))
            dve.tensor_tensor(pol[:, 0, :], chc("re"), pol[:, 10, :], ALU.mult)
            link(dve.tensor_tensor(pol[:, 1, :], chc("im"), pol[:, 10, :], ALU.mult))
            dve.tensor_tensor(pol[:, 2, :], pol[:, 0, :], pol[:, 0, :], ALU.mult)
            link(dve.tensor_tensor(pol[:, 3, :], pol[:, 1, :], pol[:, 1, :], ALU.mult))
            link(dve.tensor_tensor(pol[:, 11, :], pol[:, 2, :], pol[:, 3, :], ALU.add))
            dve.tensor_scalar(pol[:, 6, :], pol[:, 11, :], 1.0, None, ALU.max).then_inc(polar_q, 1)
            dve.wait_ge(s_win, 32)
            dve.tensor_reduce(sm[:, 16:20], winr[:, :, :], AX.X, ALU.add)
            link(dve.tensor_reduce(sm[:, 20:21], binr[:, :], AX.X, ALU.add))
            dve.scalar_tensor_tensor(out=winc[:, :, :], in0=rows(sm[:, 16:20], VC, DIM), scalar=-1.0 / DIM,
                                     in1=winr[:, :, :], op0=ALU.mult, op1=ALU.add).then_inc(win_ready, 1)
            link(dve.tensor_scalar(sm[:, 21:22], sm[:, 20:21], -1.0 / DIM, None, ALU.mult))
            link(dve.tensor_scalar(binc[:, :], binr[:, :], sm[:, 21:22], None, ALU.add))
            dve.wait_ge(polar_inv, 1)
            dve.tensor_tensor(CS[:, 0, 1, :], pol[:, 1, :], pol[:, 7, :], ALU.mult)
            dve.tensor_tensor(pol[:, 2, :], pol[:, 0, :], pol[:, 7, :], ALU.mult)
            dve.tensor_tensor(pol[:, 10, :], pol[:, 11, :], pol[:, 7, :], ALU.mult)
            link(dve.tensor_scalar(pol[:, 3, :], pol[:, 11, :], 0.5, None, ALU.is_lt))
            dve.tensor_tensor(pol[:, 8, :], pol[:, 10, :], pol[:, 4, :], ALU.mult).then_inc(polar_r, 1)
            link(dve.tensor_tensor(CS[:, 0, 0, :], pol[:, 2, :], pol[:, 3, :], ALU.add))
            dve.wait_ge(win_mean, 1)
            dve.scalar_tensor_tensor(out=wcc[:, :, :], in0=D1B[:, 0:DIM].unsqueeze(1).to_broadcast([P, VC, DIM]),
                                     scalar=-1.0 / VOCAB, in1=winc[:, :, :], op0=ALU.mult,
                                     op1=ALU.add).then_inc(win_done, 1)
            n, k = 1, 0
            while n < LEN:
                c, sn = CS[:, k, 0, :], CS[:, k, 1, :]
                lo = table[:, :, 0:n]
                dve.tensor_tensor(CS[:, 8, 0, :], c, c, ALU.mult)
                dve.tensor_tensor(CS[:, 8, 1, :], sn, sn, ALU.mult)
                if k < 7:
                    dve.scalar_tensor_tensor(out=CS[:, k + 1, 1, :], in0=c, scalar=2.0, in1=sn, op0=ALU.mult,
                                             op1=ALU.mult)
                dve.tensor_tensor(tmpA[:, :, 0:n], lo, rows(c, DEPTH, n), ALU.mult)
                link(dve.tensor_tensor(tmpB[:, :, 0:n], T2[:, :, 0:n], rows(sn, DEPTH, n), ALU.mult))
                if k < 7:
                    dve.tensor_tensor(CS[:, k + 1, 0, :], CS[:, 8, 0, :], CS[:, 8, 1, :], ALU.subtract)
                link(dve.tensor_tensor(table[:, :, n:2 * n], tmpA[:, :, 0:n], tmpB[:, :, 0:n], ALU.add))
                if 2 * n < LEN:
                    dve.tensor_tensor(tmpA[:, :, 0:n], T2[:, :, 0:n], rows(c, DEPTH, n), ALU.mult)
                    link(dve.tensor_tensor(tmpB[:, :, 0:n], lo, rows(sn, DEPTH, n), ALU.mult))
                    link(dve.tensor_tensor(T2[:, :, n:2 * n], tmpA[:, :, 0:n], tmpB[:, :, 0:n], ALU.subtract))
                n, k = 2 * n, k + 1
            dve.tensor_tensor(pol[:, 0, :], table[:, :, 1], chc("lre"), ALU.mult)
            link(dve.tensor_tensor(pol[:, 1, :], T2[:, :, 1], chc("lim"), ALU.mult))
            link(dve.tensor_tensor(pol[:, 2, :], pol[:, 0, :], pol[:, 1, :], ALU.add))
            dve.tensor_scalar(cvst[:, :, TA0], pol[:, 2, :], sgn[:, :], None, ALU.mult).then_inc(table_done, 1)

            def ffn_constants():
                dve.wait_ge(s_w2, 48)
                dve.tensor_reduce(sm[:, 24:32], w2r[:, :, :], AX.X, ALU.add)
                link(dve.tensor_reduce(sm[:, 32:32 + DEPTH], b2r[:, :, :], AX.X, ALU.add))
                dve.scalar_tensor_tensor(out=b2st[:, :, :], in0=rows(sm[:, 32:32 + DEPTH], DEPTH, DIM),
                                         scalar=-1.0 / DIM, in1=b2r[:, :, :], op0=ALU.mult,
                                         op1=ALU.add).then_inc(b2_done, 1)
                for L in range(DEPTH):
                    dve.scalar_tensor_tensor(out=ffst[:, L, 0:2 * DIM].rearrange("p (a d) -> p a d", a=2),
                                             in0=rows(sm[:, 24 + 2 * L:26 + 2 * L], 2, DIM), scalar=-1.0 / DIM,
                                             in1=w2r[:, 2 * L:2 * L + 2, :], op0=ALU.mult, op1=ALU.add)
                dve.wait_ge(b1_read, 1)
                dve.tensor_tensor(ffst[:, :, 2 * DIM:2 * DIM + 2], sm[:, 8:16].rearrange("p (l a) -> p l a", a=2),
                                  b1r[:, :].rearrange("p (l a) -> p l a", a=2), ALU.add).then_inc(ff_done, 1)

            def wo_bias():
                dve.wait_ge(bo_mm, 1)
                dve.wait_ge(s_rows, 48)
                dve.tensor_tensor(WOR[DIM:DIM + 1, :], FB[1][DIM:DIM + 1, :], WOR[DIM:DIM + 1, :],
                                  ALU.add).then_inc(wo_row, 1)
                dve.wait_ge(wo_row, 1)
                dve.tensor_reduce(sm[DIM:DIM + 1, 0:1], WOR[DIM:DIM + 1, :], AX.X, ALU.add).then_inc(sums_ready, 1)

            def input_stats(g):
                dve.wait_ge(s_x[g], 16)
                for t in range(g * GT, (g + 1) * GT):
                    dve.bn_stats(BN[:, t, :], X[:, t, :]).then_inc(bn_done, 1)
                for t in range(g * GT, (g + 1) * GT):
                    dve.wait_ge(bn_done, t + 1)
                    last = dve.bn_aggr(MV[:, t, :], BN[:, t, :])
                last.then_inc(x_stats, 1)

            def first_h(g):
                dve.wait_ge(h0_mm, g + 1)
                dve.wait_ge(x_rstd, g + 1)
                for j in range(GT):
                    t = g * GT + j
                    last = dve.scalar_tensor_tensor(out=H[:, g, j * DIM:(j + 1) * DIM],
                                                    in0=D2B[:, j * DIM:(j + 1) * DIM], scalar=RX[:, t:t + 1],
                                                    in1=binc[:, :], op0=ALU.mult, op1=ALU.add)
                last.then_inc(h0_done, 1)

            def sum_squares(u, squared, done):
                g = u % GROUPS
                dve.wait_ge(squared, u + 1)
                dve.tensor_reduce(SS[:, g, :], by_tile(SQ[:, g, :]), AX.X, ALU.add).then_inc(done, 1)

            def scale_twice(u):
                g = u % GROUPS
                dve.wait_ge(rs1, u + 1)
                dve.tensor_tensor(Z[:, g, :].rearrange("p (j a d) -> p j a d", j=GT, a=2),
                                  by_tile(H[:, g, :]).unsqueeze(2).to_broadcast([P, GT, 2, DIM]),
                                  RS[:, g, :].unsqueeze(2).unsqueeze(3).to_broadcast([P, GT, 2, DIM]),
                                  ALU.mult).then_inc(z1, 1)

            def scale(u, ready, done):
                g = u % GROUPS
                dve.wait_ge(ready, u + 1)
                dve.tensor_tensor(by_tile(Z[:, g, 0:HC]), by_tile(H[:, g, :]), rows(RS[:, g, :], GT, DIM),
                                  ALU.mult).then_inc(done, 1)

            def modulate(u):
                g, L = u % GROUPS, u // GROUPS
                dve.wait_ge(y1, u + 1)
                if u == 0:
                    dve.wait_ge(table_done, 1)
                dve.tensor_tensor(by_seq(U[:, g, :]), by_seq(Y[:, g, :]),
                                  cvst[:, L, TA0:TA0 + SL].unsqueeze(1).to_broadcast([P, SG, SL]),
                                  ALU.mult).then_inc(u1, 1)

            def scan(u):
                g, L = u % GROUPS, u // GROUPS
                dve.wait_ge(u1, u + 1)
                if u == 0:
                    dve.wait_ge(cv_store, 2)
                dve.tensor_tensor_scan(V[:, g, :], cvst[:, L, DC0:DC0 + UC], U[:, g, :], 0.0, ALU.mult,
                                       ALU.add).then_inc(v1, 1)

            def demodulate(u):
                g, L = u % GROUPS, u // GROUPS
                dve.wait_ge(v1, u + 1)
                dve.tensor_tensor(by_seq(U[:, g, 0:GW]), by_seq(V[:, g, :])[:, :, 1:SL],
                                  cvst[:, L, TA0 + 1:TA0 + SL].unsqueeze(1).to_broadcast([P, SG, LEN]),
                                  ALU.mult).then_inc(w1, 1)

            def add_conv(u):
                g = u % GROUPS
                dve.wait_ge(d1, u + 1)
                dve.tensor_tensor(H[:, g, :], D1B[:, 0:HC], H[:, g, :], ALU.add).then_inc(a1, 1)

            def add_ffn(u):
                g = u % GROUPS
                dve.wait_ge(d2, u + 1)
                dve.wait_ge(hb, u + 1)
                dve.tensor_tensor(H[:, g, :], D2B[:, 0:HC], HB[:, g, :], ALU.add).then_inc(a2, 1)

            def step(s):
                conv = 0 <= s - 1 < UNITS
                if conv:
                    scan(s - 1)
                sum_squares(s, sq1, ss1)
                if 0 <= s - 2 < UNITS:
                    scale(s - 2, rs2, z2)
                if conv:
                    demodulate(s - 1)
                if 0 <= s - 3 < UNITS:
                    add_ffn(s - 3)
                if s + 1 < GROUPS:
                    input_stats(s + 1)
                if s < UNITS:
                    scale_twice(s)
                else:
                    scale(s, rs1, z1)
                if s == 1:
                    ffn_constants()
                if conv:
                    add_conv(s - 1)
                    sum_squares(s - 1, sq2, ss2)
                if s == 1:
                    wo_bias()
                if s + 1 < GROUPS:
                    first_h(s + 1)
                if s < UNITS:
                    modulate(s)

            def first_result(t):
                dve.wait_ge(o_rstd, t // 2 + 1)
                dve.scalar_tensor_tensor(out=X[:, t, :], in0=OB[t % 2][:, :], scalar=OR[:, t:t + 1],
                                         in1=X[:, t, :], op0=ALU.mult, op1=ALU.add).then_inc(x1_done, 1)

            def first_stats(t):
                dve.wait_ge(x1_done, t + 1)
                dve.bn_stats(BN[:, t, :], X[:, t, :]).then_inc(bn1_done, 1)

            def first_mean(t):
                dve.wait_ge(bn1_done, t + 1)
                dve.bn_aggr(MV1[:, t, :], BN[:, t, :]).then_inc(mv1_done, 1)

            def normalise(t):
                dve.wait_ge(r1_ready, t // 2 + 1)
                dve.tensor_scalar(XN[:, t, :], X[:, t, :], MV1[:, t, 0:1], R1X[:, t:t + 1], ALU.subtract,
                                  ALU.mult).then_inc(xn_done, 1)

            def select_pair(t0):
                for t in (t0, t0 + 1):
                    dve.wait_ge(gelu_done, t + 1)
                    dve.max(M8[:, t % 2, :], SBK[t % 4][:, 0:NSLOT]).then_inc(top_found, 1)
                for t in (t0, t0 + 1):
                    dve.scalar_tensor_tensor(out=GJ[:, t % 2, :], in0=GE[:, t % 4, :], scalar=1.0, in1=ltc("wu2"),
                                             op0=ALU.mult, op1=ALU.mult, accum_out=LRN[:, t:t + 1]) \
                        .then_inc(lrn_done, 1)
                    dve.wait_ge(top_found, t + 1)
                    dve.match_replace(REP[:, t % 4, :], M8[:, t % 2, :], SBK[t % 4][:, 0:NSLOT],
                                      LOWEST).then_inc(top_marked, 1)
                q = t0 % 4
                dve.wait_ge(top_marked, t0 + 2)
                dve.tensor_scalar(OFS[:, q:q + 2, :], REP[:, q:q + 2, :], LOWEST, -BIG, ALU.not_equal,
                                  ALU.mult).then_inc(top_ofs, 1)
                dve.wait_ge(top_ofs, t0 // 2 + 1)
                for t in (t0, t0 + 1):
                    dve.tensor_tensor(AM[:, t, :], SBK[t % 4][:, NSLOT:2 * NSLOT], OFS[:, t % 4, :],
                                      ALU.add).then_inc(sc_read, 1)

            def group_max(g):
                dve.wait_ge(sc_read, GT * g + GT)
                dve.tensor_reduce(NMX[:, GT * g:GT * g + GT], AM[:, GT * g:GT * g + GT, :], AX.X, ALU.max,
                                  negate=True).then_inc(am_max, 1)

            input_stats(0)
            first_h(0)
            for s in range(STEPS - EARLY):
                step(s)
            for k in range(PAIRS + LAG + 1):
                if k < EARLY:
                    step(STEPS - EARLY + k)
                back = 2 * (k - LAG - 1)
                if 0 <= k - 1 < PAIRS:
                    a, b = 2 * k - 2, 2 * k - 1
                    first_result(a)
                    first_result(b)
                    first_stats(a)
                    first_stats(b)
                    first_mean(a)
                    first_mean(b)
                if back >= 0:
                    select_pair(back)
                    if back % 4 == 2:
                        group_max(back // 4)
                if 0 <= k - 1 < PAIRS:
                    normalise(2 * k - 2)
                    normalise(2 * k - 1)

            steps = [0]

            def gstep(ins):
                steps[0] += 1
                ins.then_inc(ga_step, 1)
                dve.wait_ge(ga_step, steps[0])

            dve.tensor_scalar(GA[:, 8, :], LRN[:, :], ltc("bu2"), -80.0, ALU.add, ALU.max).then_inc(sig_in, 1)
            gstep(dve.tensor_tensor(GA[:, 0, :], R1X[:, :], R1X[:, :], ALU.mult))
            gstep(dve.tensor_tensor(GA[:, 1, :], GA[:, 0, :], MV1[:, :, 1], ALU.mult))
            dve.tensor_scalar(GA[:, 2, :], GA[:, 1, :], 1.0, None, ALU.add).then_inc(ln_in, 1)
            dve.wait_ge(ln_in, 1)
            gstep(dve.tensor_scalar(GA[:, 4, :], GA[:, 2, :], 1.0, None, ALU.subtract))
            gstep(dve.tensor_scalar(GA[:, 5, :], GA[:, 4, :], 0.0, None, ALU.is_equal))
            gstep(dve.tensor_tensor(GA[:, 6, :], GA[:, 4, :], GA[:, 5, :], ALU.add))
            dve.tensor_tensor(GA[:, 11, :], GA[:, 5, :], GA[:, 1, :], ALU.mult)
            gstep(dve.reciprocal(GA[:, 7, :], GA[:, 6, :]))
            gstep(dve.tensor_tensor(GA[:, 10, :], GA[:, 7, :], GA[:, 1, :], ALU.mult))
            dve.wait_ge(ln_out, 1)
            gstep(dve.tensor_tensor(GA[:, 12, :], GA[:, 3, :], GA[:, 10, :], ALU.mult))
            gstep(dve.tensor_tensor(GA[:, 13, :], GA[:, 12, :], GA[:, 11, :], ALU.add))
            dve.tensor_reduce(gsum[:, 0:1], GA[:, 13, :], AX.X, ALU.add).then_inc(gsum_in, 1)
            dve.wait_ge(sig_out, 1)
            gstep(dve.tensor_scalar(GA[:, 17, :], GA[:, 9, :], 1.0, None, ALU.add))
            gstep(dve.reciprocal(GA[:, 18, :], GA[:, 17, :]))
            dve.wait_ge(gsum_mm, 1)
            gstep(dve.tensor_scalar(gsum[:, 1:2], D1B[:, 0:1], 1.0 / TOK, 1e-6, ALU.mult, ALU.add))
            gstep(dve.reciprocal(gsum[:, 2:3], gsum[:, 1:2]))
            gstep(dve.tensor_scalar(GA[:, 14, :], GA[:, 13, :], gsum[:, 2:3], 0.5, ALU.mult, ALU.mult))
            gstep(dve.scalar_tensor_tensor(out=GA[:, 19, :], in0=GA[:, 18, :], scalar=2.5, in1=GA[:, 14, :],
                                           op0=ALU.mult, op1=ALU.add))
            gstep(dve.tensor_scalar(GA[:, 20, :], GA[:, 19, :], 0.0, 5.0, ALU.max, ALU.min))
            gstep(dve.tensor_scalar(GA[:, 21, :], GA[:, 20, :], 0.5, 1.0 / 1.5, ALU.subtract, ALU.mult))
            gstep(dve.tensor_scalar(GA[:, 22, :], GA[:, 21, :], 0.0, 1.0, ALU.max, ALU.min))
            gstep(dve.tensor_scalar(GA[:, 23, :], GA[:, 22, :], ltc("gw"), ltc("gb"), ALU.mult, ALU.add))
            dve.tensor_scalar(GA[:, 15, :], GA[:, 23, :], -80.0, None, ALU.max).then_inc(gate_in, 1)
            dve.wait_ge(gate_out, 1)
            gstep(dve.tensor_scalar(GA[:, 0, :], GA[:, 16, :], 1.0, None, ALU.add))
            gstep(dve.reciprocal(GA[:, 1, :], GA[:, 0, :]))
            gstep(dve.scalar_tensor_tensor(out=GA[:, 4, :], in0=GA[:, 1, :], scalar=0.05, in1=GA[:, 1, :],
                                           op0=ALU.is_ge, op1=ALU.mult))

            def weigh(k):
                a, b = 2 * k, 2 * k + 2
                dve.wait_ge(e_ready, b)
                dve.reciprocal(RES[:, a:b], ES[:, a:b]).then_inc(es_inv, 1)
                dve.wait_ge(es_inv, k + 1)
                dve.tensor_tensor(GS[:, a:b], RES[:, a:b], GA[:, 4, a:b], ALU.mult).then_inc(gs_ready, 1)

            def mix(t):
                dve.wait_ge(gs_ready, t // 2 + 1)
                dve.wait_ge(aux_mm, t + 1)
                dve.scalar_tensor_tensor(out=XN[:, t, :], in0=FB[t % 4][:, :], scalar=GS[:, t:t + 1],
                                         in1=XN[:, t, :], op0=ALU.mult, op1=ALU.add).then_inc(zz_ready, 1)

            def finish(t):
                dve.wait_ge(z_rstd, t // 2 + 1)
                dve.scalar_tensor_tensor(out=X[:, t, :], in0=XN[:, t, :], scalar=ZR[:, t:t + 1],
                                         in1=X[:, t, :], op0=ALU.mult, op1=ALU.add).then_inc(out_ready, 1)

            for k in range(PAIRS + 2):
                if k < PAIRS:
                    weigh(k)
                    mix(2 * k)
                    mix(2 * k + 1)
                if k >= 2:
                    finish(2 * k - 4)
                    finish(2 * k - 3)

        @block.tensor
        def _(pe):
            pe.wait_ge(pool_const, 1)
            pe.wait_ge(win_ready, 1)
            for c in range(VC):
                last = pe.matmul(D1B[:, 0:DIM], ones[:, :], winc[:, c, :], start=(c == 0), stop=(c == VC - 1))
            last.then_inc(win_mean, 1)

            def setup_ffn():
                pe.wait_ge(s_c64, 16)
                for k in range(2 * DEPTH):
                    last = pe.matmul(FB[0][:, k:k + 1], c6c("w1t", k * P, (k + 1) * P),
                                     c6c("b2", k // 2, k // 2 + 1), start=True, stop=True)
                last.then_inc(b1_mm, 1)
                pe.wait_ge(act_step, 1)
                pe.matmul(FB[1][0:DIM + 1, :], lbp[:, :], c6c("wout"), start=True, stop=True).then_inc(bo_mm, 1)

            def setup_late():
                pe.matmul(FB[2][0:RDIM, 0:NSLOT], c6c("wrt"), c6c("keys"), start=True, stop=True).then_inc(rk_mm, 1)
                pe.wait_ge(s_late, 48)
                vals = ltc("vals").rearrange("p (c n) -> p c n", c=VC)
                wvd = ltc("wvd").rearrange("p (c n) -> p c n", c=VC)
                for c in range(VC):
                    last = pe.matmul(FB[3][0:VB, 0:NSLOT], wvd[:, c, :], vals[:, c, :], start=(c == 0),
                                     stop=(c == VC - 1))
                last.then_inc(vp_mm, 1)
                pe.wait_ge(rk_sb, 1)
                pe.wait_ge(b1_read, 1)
                pe.matmul(FB[0][0:BOT, 0:NSLOT], wr_s[:, :], rkT[:, :], start=True, stop=True).then_inc(g_mm, 1)
                pe.wait_ge(vp_sb, 1)
                pe.matmul(FB[2][:, :], vpT[:, :], wvu_s[:, :], start=True, stop=True).then_inc(v2_mm, 1)
                pe.wait_ge(kb_sb, 1)
                for c in range(VC):
                    last = pe.matmul(FB[0 if c < 2 else 3][:, (c % 2) * 2 * NSLOT:(c % 2 + 1) * 2 * NSLOT],
                                     c6c("wq", c * P, (c + 1) * P), KB[:, :], start=True, stop=True)
                    if c % 2:
                        last.then_inc(sw_mm, 1)

            def first_h(g):
                pe.wait_ge(s_xt[g], 16)
                if g == 0:
                    pe.wait_ge(win_done, 1)
                else:
                    pe.wait_ge(h0_done, g)
                for j in range(GT):
                    for c in range(VC):
                        last = pe.matmul(D2B[:, j * DIM:(j + 1) * DIM], XT[:, g, c, j * P:(j + 1) * P],
                                         wcc[:, c, :], start=(c == 0), stop=(c == VC - 1))
                last.then_inc(h0_mm, 1)

            def turn1(u):
                g = u % GROUPS
                pe.wait_ge(z1, u + 1)
                if u >= 1:
                    pe.wait_ge(y1, u)
                for j in range(GT):
                    if u < UNITS:
                        last = pe.transpose(T1B[:, j * P:(j + 1) * P], Z[:, g, j * P:(j + 1) * P], ident[:, :])
                    else:
                        last = pe.transpose(T1B[0:DIM, j * P:(j + 1) * P], Z[:, g, j * DIM:(j + 1) * DIM],
                                            ident[:, :])
                last.then_inc(t1, 1)

            def mix_in(u):
                g, L = u % GROUPS, u // GROUPS
                pe.wait_ge(w1, u + 1)
                if u == 0:
                    pe.wait_ge(cv_store, 1)
                else:
                    pe.wait_ge(a1, u)
                for j in range(GT):
                    last = pe.matmul(D1B[:, j * DIM:(j + 1) * DIM], U[:, g, j * P:(j + 1) * P],
                                     cvst[:, L, MX0:MX0 + DIM], start=True, stop=True)
                last.then_inc(d1, 1)

            def turn2(u):
                g = u % GROUPS
                pe.wait_ge(z2, u + 1)
                if u >= 1:
                    pe.wait_ge(e2, u)
                for j in range(GT):
                    last = pe.transpose(T2B[0:DIM, j * P:(j + 1) * P], Z[:, g, j * DIM:(j + 1) * DIM], ident[:, :])
                last.then_inc(t2, 1)

            def hidden(u, a):
                g, L = u % GROUPS, u // GROUPS
                pe.wait_ge(e2, u + 1)
                if a == 0 and g == 0:
                    pe.wait_ge(w1_store, L + 1)
                if u < 2:
                    pe.wait_ge(sw_read, 2)
                    pe.wait_ge(wo_row, 1)
                else:
                    pe.wait_ge(g2, 2 * u + a - 3)
                pe.matmul(FB[(2 * u + a) % 4][:, :], w1st[:, L, a * P:(a + 1) * P], Z2[:, g, :], start=True,
                          stop=True).then_inc(f2, 1)

            def project(u):
                g, L = u % GROUPS, u // GROUPS
                pe.wait_ge(g2, 2 * u + 2)
                if u == 0:
                    pe.wait_ge(h0_done, GROUPS)
                else:
                    pe.wait_ge(a2, u)
                for j in range(GT):
                    for a in range(2):
                        last = pe.matmul(D2B[:, j * DIM:(j + 1) * DIM], HD[:, u % 2, a, j * P:(j + 1) * P],
                                         ffst[:, L, a * DIM:(a + 1) * DIM], start=(a == 0), stop=(a == 1))
                last.then_inc(d2, 1)

            def step(s):
                if 0 <= s - 3 < UNITS:
                    project(s - 3)
                ffn = 0 <= s - 2 < UNITS
                if ffn:
                    turn2(s - 2)
                if 0 <= s - 1 < UNITS:
                    mix_in(s - 1)
                if ffn:
                    hidden(s - 2, 0)
                turn1(s)
                if s + 1 < GROUPS:
                    first_h(s + 1)
                if ffn:
                    hidden(s - 2, 1)

            def output(t):
                if t == 0:
                    pe.wait_ge(late_ready, 1)
                    pe.wait_ge(g2, 2 * UNITS)
                pe.wait_ge(y1, UNITS + t // GT + 1)
                if t >= 2:
                    pe.wait_ge(x1_done, t - 1)
                pe.matmul(OB[t % 2][:, :], Z2[:, t // GT, (t % GT) * P:(t % GT + 1) * P], WO[:, :], start=True,
                          stop=True).then_inc(o_mm, 1)

            def turn_xn(t):
                pe.wait_ge(xn_done, t + 1)
                if t >= 2:
                    pe.wait_ge(xtr_read, t - 1)
                else:
                    pe.wait_ge(y1, STEPS)
                    pe.wait_ge(e2, UNITS)
                for c in range(VC):
                    last = pe.transpose(bank[t % 2][:, c * P:(c + 1) * P], XN[:, t, c * P:(c + 1) * P], ident[:, :])
                last.then_inc(xtr, 1)

            def scores(t):
                pe.wait_ge(xtr_read, t + 1)
                if t >= 4:
                    pe.wait_ge(sc_read, t - 3)
                else:
                    pe.wait_ge(a1, UNITS)
                    pe.wait_ge(a2, UNITS)
                    pe.wait_ge(sw_read, 2)
                    pe.wait_ge(s_rows, 48)
                pe.matmul(SBK[t % 4][:, 0:SW], ones[0:1, :], SWR[:, :], start=True, stop=False)
                for c in range(VC):
                    last = pe.matmul(SBK[t % 4][:, 0:SW], XNT[:, t % 4, c * P:(c + 1) * P], SW_[:, c, :],
                                     start=False, stop=(c == VC - 1))
                last.then_inc(s_mm, 1)

            first_h(0)
            for s in range(STEPS - EARLY):
                if s == 1:
                    setup_ffn()
                    setup_late()
                step(s)
            for k in range(PAIRS + LAG):
                if k < EARLY:
                    step(STEPS - EARLY + k)
                back = 2 * (k - LAG)
                if back >= 0:
                    turn_xn(back)
                    turn_xn(back + 1)
                for j in range(2):
                    if k < PAIRS:
                        output(2 * k + j)
                    if back >= 0:
                        scores(back + j)
            pe.wait_ge(sc_read, TILES)
            pe.wait_ge(gsum_in, 1)
            pe.matmul(D1B[:, 0:1], ones[:, :], gsum[:, 0:1], start=True, stop=True).then_inc(gsum_mm, 1)

            def turn_e(k):
                pe.wait_ge(e_ready, 2 * k + 2)
                if k >= 2:
                    pe.wait_ge(et_ready, k - 1)
                for j in range(2):
                    last = pe.transpose(bank[k % 2][:, j * P:(j + 1) * P], E_[:, k % 2, j * P:(j + 1) * P],
                                        ident[:, :])
                last.then_inc(e_tr, 1)

            def memory(t):
                pe.wait_ge(et_ready, t // 2 + 1)
                if t >= 4:
                    pe.wait_ge(zz_ready, t - 3)
                pe.matmul(FB[t % 4][:, :], ET[:, t // 2 % 2, (t % 2) * P:(t % 2 + 1) * P], V2[:, :], start=True,
                          stop=True).then_inc(aux_mm, 1)

            for k in range(PAIRS + 1):
                if k < PAIRS:
                    turn_e(k)
                if k >= 1:
                    memory(2 * k - 2)
                    memory(2 * k - 1)


def kernel(**inputs):
    import concourse.bacc as bacc
    from concourse import mybir as _mybir
    from concourse.bass_utils import run_bass_kernel_spmd

    a = {k.split("_", 2)[2] if k.startswith("L0_attn_") else k[7:]: np.asarray(v) for k, v in inputs.items()}

    def chunks(w):
        return w.T.reshape(VC, P, w.shape[0]).transpose(1, 0, 2)

    def twice(v):
        return np.concatenate([v.T, v.T], axis=0)

    def column(v):
        return np.broadcast_to(v.reshape(1, 1), (P, 1))

    x = a["x"].reshape(TOK, VOCAB)
    xT = x.reshape(GROUPS, GW, VC, P).transpose(3, 0, 2, 1)
    late = [chunks(a["aux_values"]), chunks(a["Wvd"]), np.broadcast_to(a["Wu2"], (P, UH)), column(a["bu2"]), column(a["gate_w1"]), column(a["gate_bias"])]
    c64 = [a["ln2_w"].T, a["ln2_b"].T, a["lnl_w"].reshape(DIM, 1), a["lnl_b"].reshape(DIM, 1),
           a["W1"].transpose(2, 0, 1).reshape(DIM, DEPTH * DFF), a["Wout"].T, a["Wr"].T, a["aux_keys"].T,
           a["Wq"]]
    arrays = {
        "x": x, "xT": xT, "win": chunks(a["Win"]),
        "binb": np.broadcast_to(a["bin"], (P, DIM)),
        "ch": np.concatenate([twice(a[n]) for n in ("phz_re", "phz_im", "lc_re", "lc_im", "sc_lin", "ln1_w", "ln1_b")],
                             axis=1),
        "c64": np.concatenate(c64, axis=1),
        "w2t": a["W2"].reshape(DEPTH, DIM, 2, P).transpose(3, 0, 2, 1).reshape(P, 2 * DEPTH, DIM),
        "b1": a["b1"].reshape(DEPTH * 2, P).T,
        "b2b": np.broadcast_to(a["b2"], (P, DEPTH, DIM)),
        "late": np.concatenate([v.reshape(P, -1) for v in late], axis=1),
        "wu1": chunks(a["Wu1"]), "wr": a["Wr"], "wvu": a["Wvu"].T, "boutr": a["bout"].reshape(1, VOCAB), 
        "srow": np.concatenate([a["log_rel"], a["log_rel"], a["bu1"]]).reshape(1, SW),
    }
    arrays = {k: np.ascontiguousarray(v) for k, v in arrays.items()}
    nc = bacc.Bacc("TRN2", target_bir_lowering=False, num_devices=1)
    args = [nc.dram_tensor(f"in_{k}", v.shape, _mybir.dt.from_np(v.dtype), kind="ExternalInput").ap()
            for k, v in arrays.items()]
    args.append(nc.dram_tensor("out_0", (TOK, VOCAB), _mybir.dt.float32, kind="ExternalOutput").ap())
    build(nc, *args)
    r = run_bass_kernel_spmd(nc, [{f"in_{k}": v for k, v in arrays.items()}], core_ids=[0])
    return r.results[0]["out_0"].reshape(SEQS, LEN, VOCAB)
```

```python
from contextlib import ExitStack

import numpy as np
from concourse import mybir

ALU = mybir.AluOpType
ACT = mybir.ActivationFunctionType
AX = mybir.AxisListType
F32, BF16 = mybir.dt.float32, mybir.dt.bfloat16

P = 128
DEPTH, DIM, DFF, VOCAB = 4, 64, 256, 512
SEQS, LEN = 8, 256
TOK = SEQS * LEN
TILES = TOK // P
GT = 4
GROUPS = TILES // GT
GW = GT * P
SG = GW // LEN
SL = LEN + 1
UC = SG * SL
HC = GT * DIM
VC = VOCAB // P
BOT, RDIM, NSLOT, VB, UH = 64, 48, 128, 32, 128
EPS = 1e-5
TINY = 1e-30
BIG = 1e30
LOWEST = -3e38
UNITS = DEPTH * GROUPS
SW = 2 * NSLOT + UH

CH = {n: i * DEPTH for i, n in enumerate(["re", "im", "lre", "lim", "scl", "w", "b"])}
CHN = 7 * DEPTH
LATE = {}
_at = 0
for _n, _k in (("vals", VC * NSLOT), ("wvd", VC * VB), ("wu2", UH), ("bu2", 1), ("gw", 1), ("gb", 1)):
    LATE[_n] = (_at, _at + _k)
    _at += _k
LATEN = _at
C64 = {}
_at = 0
for _n, _k in (("w2", DEPTH), ("b2", DEPTH), ("lw", 1), ("lb", 1), ("w1t", DEPTH * DFF), ("wout", VOCAB),
               ("wrt", RDIM), ("keys", NSLOT), ("wq", VOCAB)):
    C64[_n] = (_at, _at + _k)
    _at += _k
C64N = _at
TA0 = 0
T20 = TA0 + SL
MX0 = T20 + LEN // 2
LW0 = MX0 + P
LB0, DC0 = LW0 + 1, LW0 + 2
NCV = DC0 + UC
NFF = 2 * P + 2
PAIRS = TILES // 2
ROWS = 3 * 32


def build(nc, x, xT, win, binb, ch, c64, w2t, b1, b2b, late, wu1, wr, wvu, boutr, srow, out):
    with ExitStack() as ctx:
        def sb(name, shape, dtype=F32):
            return ctx.enter_context(nc.sbuf_tensor(name, shape, dtype))

        def sem(name):
            return ctx.enter_context(nc.semaphore(name))

        X = sb("X", [P, TILES, VOCAB])
        XT = sb("XT", [P, GROUPS, VC, GW])
        XN = XT[:, :, :, :].rearrange("p g c t -> p (g c) t")
        H = sb("H", [P, GROUPS, HC])
        HB = sb("HB", [P, GROUPS, HC])
        ident = sb("ident", [P, P])
        ones = sb("ones", [P, P])
        nhalf = sb("nhalf", [P, GT])
        epst = sb("epst", [P, GT])
        centre = sb("centre", [P, DIM])
        winr = sb("winr", [P, VC, DIM])
        binr = sb("binr", [P, DIM])
        chp = sb("chp", [P, CHN])
        c6 = sb("c6", [DIM, C64N])
        w2r = sb("w2r", [P, DEPTH * 2, DIM])
        b1r = sb("b1r", [P, DEPTH * 2])
        b2r = sb("b2r", [P, DEPTH, DIM])
        lt = sb("lt", [P, LATEN])
        wr_s = sb("wr_s", [RDIM, BOT])
        wvu_s = sb("wvu_s", [VB, VOCAB])
        winc = sb("winc", [P, VC, DIM])
        wcc = sb("wcc", [P, VC, P])
        binc = sb("binc", [P, DIM])
        cvst = sb("cvst", [P, DEPTH, NCV])
        ffst = sb("ffst", [P, DEPTH, NFF])
        w1st = sb("w1st", [P, DEPTH, DFF])
        b2st = sb("b2st", [P, DEPTH, DIM])
        tmpA = sb("tmpA", [P, DEPTH, LEN // 2])
        tmpB = sb("tmpB", [P, DEPTH, LEN // 2])
        CS = sb("CS", [P, 9, 3, DEPTH])
        pol = sb("pol", [P, 12, DEPTH])
        WO = sb("WO", [P, VOCAB])
        WOR = sb("WOR", [DIM + 1, VOCAB])
        KB = sb("KB", [BOT, 2 * NSLOT])
        SW_ = sb("SW_", [P, VC, SW])
        SWR = sb("SWR", [ROWS, SW])
        SWD = sb("SWD", [ROWS, SW])
        SWB = sb("SWB", [ROWS, SW], BF16)
        pick = sb("pick", [ROWS, P], BF16)
        V2 = sb("V2", [NSLOT, VOCAB])
        V2R = sb("V2R", [NSLOT, VOCAB])
        lbp = sb("lbp", [DIM, DIM + 1])
        rkT = sb("rkT", [RDIM, NSLOT])
        vpT = sb("vpT", [VB, NSLOT])
        sm = sb("sm", [P, 64])
        SQ = sb("SQ", [P, GROUPS, HC])
        SS = sb("SS", [P, GROUPS, GT])
        VE = sb("VE", [P, GROUPS, GT])
        RS = sb("RS", [P, GROUPS, GT])
        Z = sb("Z", [P, GROUPS, 2 * HC])
        Y = sb("Y", [P, GROUPS, UC])
        U = sb("U", [P, GROUPS, UC])
        V = sb("V", [P, GROUPS, UC])
        Z2 = sb("Z2", [P, GROUPS, GW])
        HD = sb("HD", [P, 2, 2, GW])
        BN = sb("BN", [P, TILES, 6])
        MV = sb("MV", [P, TILES, 2])
        VX, RX, OSQ, OV, OR, V1X, R1X, LRN, NMX, ES, GS, RES, ZQ, ZV, ZR = (
            sb(n, [P, TILES]) for n in ("VX", "RX", "OSQ", "OV", "OR", "V1X", "R1X", "LRN", "NMX", "ES", "GS",
                                        "RES", "ZQ", "ZV", "ZR"))
        MV1 = sb("MV1", [P, TILES, 2])
        M8 = sb("M8", [P, 2, 8])
        GA = sb("GA", [P, 24, TILES])
        gsum = sb("gsum", [P, 4])
        REP, OFS = tmpA, tmpB
        AM = cvst[:, :, :].rearrange("p l n -> p (l n)")[:, 0:TILES * NSLOT].rearrange("p (t n) -> p t n", t=TILES)
        XNT = Y
        GE = V[:, 0, 0:4 * UH].rearrange("p (t n) -> p t n", t=4)
        GJ = V[:, 1, 0:2 * UH].rearrange("p (t n) -> p t n", t=2)
        JK = V[:, 2:4, 0:GW]
        E_ = U[:, 0:2, 0:2 * NSLOT]
        ET = U[:, 2:4, 0:2 * P]

        bank = [ctx.enter_context(nc.psum_tensor(f"bank{i}", [P, 512], F32)) for i in range(8)]
        T1B, T2B = bank[0], bank[1]
        FB = bank[2:5]
        LB = bank[5]
        HB0 = bank[2:6]
        D1B, D2B = bank[6], bank[7]
        XB = [bank[1], bank[0]]
        OB = bank[5:7]
        SBK = [bank[2], bank[3], bank[4], bank[7]]
        MB = [bank[5], bank[6], bank[2], bank[3]]

        s_ch, s_win, s_c64, s_w2, s_late, s_rows = (sem(n) for n in (
            "s_ch", "s_win", "s_c64", "s_w2", "s_late", "s_rows"))
        s_xt = [sem(f"s_xt{g}") for g in range(GROUPS)]
        s_x = [sem(f"s_x{g}") for g in range(GROUPS)]
        pool_const = sem("pool_const")
        pool_zero = sem("pool_zero")
        pool_step = sem("pool_step")
        polar_q, polar_inv = sem("polar_q"), sem("polar_inv")
        polar_r, decay = sem("polar_r"), sem("decay")
        dve_step = sem("dve_step")
        win_ready, win_mean, win_done = sem("win_ready"), sem("win_mean"), sem("win_done")
        b1_mm, b1_read, act_step = sem("b1_mm"), sem("b1_read"), sem("act_step")
        wo_row, sums_ready, sums_scaled = sem("wo_row"), sem("sums_ready"), sem("sums_scaled")
        cv_store, table_done, ff_done, b2_done = sem("cv_store"), sem("table_done"), sem("ff_done"), sem("b2_done")
        pool_out = sem("pool_out")
        state_done, rows_done = sem("state_done"), sem("rows_done")
        late_mm, late_read = sem("late_mm"), sem("late_read")
        w1_store = sem("w1_store")
        late_ready = sem("late_ready")
        x_stats, x_ve, x_rstd, bn_done, h0_mm, h0_done = (sem(n) for n in (
            "x_stats", "x_ve", "x_rstd", "bn_done", "h0_mm", "h0_done"))
        sq1, ss1, ve1, rs1, z1, t1, y1, u1, v1, w1, d1, a1 = (sem(n + "1") for n in (
            "squared", "sumsq", "vareps", "rstd", "z", "turned", "y", "u", "v", "w", "delta", "h_added"))
        sq2, ss2, ve2, rs2, z2, t2, e2, f2, g2, d2, a2 = (sem(n + "2") for n in (
            "squared", "sumsq", "vareps", "rstd", "z", "turned", "z_out", "hidden", "silu", "delta", "h_added"))
        hb = sem("hb")
        o_mm, o_sq, o_ve, o_rstd, x1_done = (sem(n) for n in ("o_mm", "o_sq", "o_ve", "o_rstd", "x1_done"))
        bn1_done, mv1_done, v1_ve, r1_ready, xn_done, xtr, xtr_read = (sem(n) for n in (
            "bn1_done", "mv1_done", "v1_ve", "r1_ready", "xn_done", "xtr", "xtr_read"))
        s_mm, gelu_done, lrn_done, top_found, top_marked, top_ofs, sc_read, am_max = (sem(n) for n in (
            "s_mm", "gelu_done", "lrn_done", "top_found", "top_marked", "top_ofs", "sc_read", "am_max"))
        ga_step, ln_in, ln_out, gsum_in, gsum_mm, gsum_read, sig_in, sig_out, gate_in, gate_out = (sem(n) for n in (
            "ga_step", "ln_in", "ln_out", "gsum_in", "gsum_mm", "gsum_read", "sig_in", "sig_out", "gate_in", "gate_out"))
        e_ready, e_tr, et_ready, aux_mm, es_inv, gs_ready, zz_ready, z_sq, z_ve, z_rstd, out_ready, s_out = (
            sem(n) for n in ("e_ready", "e_tr", "et_ready", "aux_mm", "es_inv", "gs_ready", "zz_ready", "z_sq",
                             "z_ve", "z_rstd", "out_ready", "s_out"))

        def c6c(name, a=0, b=None):
            lo, hi = C64[name]
            return c6[:, lo + a:(hi if b is None else lo + b)]

        def ltc(name):
            return lt[:, LATE[name][0]:LATE[name][1]]

        def chc(name):
            return chp[:, CH[name]:CH[name] + DEPTH]

        def rows(ap, n, w):
            return ap.unsqueeze(2).to_broadcast([ap.shape[0], n, w])

        def by_tile(ap):
            return ap.rearrange("p (j d) -> p j d", j=GT)

        def by_seq(ap):
            return ap.rearrange("p (s l) -> p s l", s=SG)

        x_v = x.rearrange("(g j p) v -> g p j v", p=P, j=GT)
        out_v = out.rearrange("(k j p) v -> k p j v", p=P, j=2)
        table = cvst[:, :, TA0 + 1:TA0 + SL]
        T2 = cvst[:, :, T20:T20 + LEN // 2]
        both = cvst[:, :, TA0 + 1:TA0 + 1 + 2 * LEN].rearrange("p l (a n) -> p l a n", a=2)
        STEPS = UNITS + GROUPS
        EARLY = 2
        LATE0, LATES = 4, 7
        POOL_TILES = (1, 4, 7, 10)
        LAG = 2

        block = ctx.enter_context(nc.Block())

        @block.sync
        def _(sp):
            sp.dma_start(winr[:, :, :], win).then_inc(s_win, 16)
            sp.dma_start(binr[:, :], binb).then_inc(s_win, 16)
            sp.dma_start(chp[:, :], ch).then_inc(s_ch, 16)
            for g in range(GROUPS):
                sp.dma_start(XT[:, g, :, :], xT[:, g]).then_inc(s_xt[g], 16)
                sp.dma_start(X[:, g * GT:(g + 1) * GT, :], x_v[g]).then_inc(s_x[g], 16)
                if g == 0:
                    sp.dma_start(c6[:, :], c64).then_inc(s_c64, 16)
                if g == 1:
                    sp.dma_start(w2r[:, :, :], w2t).then_inc(s_w2, 16)
                    sp.dma_start(b1r[:, :], b1).then_inc(s_w2, 16)
                    sp.dma_start(b2r[:, :, :], b2b).then_inc(s_w2, 16)
                if g == 3:
                    sp.dma_start(lt[:, :], late).then_inc(s_late, 16)
                    sp.dma_start(wr_s[:, :], wr).then_inc(s_late, 16)
                    sp.dma_start(wvu_s[:, :], wvu).then_inc(s_late, 16)
                    sp.dma_start(WOR[DIM:DIM + 1, :], boutr).then_inc(s_rows, 16)
                    sp.dma_start(SWR[:, :], srow).then_inc(s_rows, 16)
                    sp.dma_start(SW_[:, :, 2 * NSLOT:SW], wu1).then_inc(s_rows, 16)
            for k in range(PAIRS):
                sp.wait_ge(out_ready, sum(t not in POOL_TILES for t in range(2 * k + 2)))
                if any(t in POOL_TILES for t in (2 * k, 2 * k + 1)):
                    sp.wait_ge(pool_out, 2 * sum(t < 2 * k + 2 for t in POOL_TILES))
                sp.dma_start(out_v[k], X[:, 2 * k:2 * k + 2, :]).then_inc(s_out, 16)
            sp.wait_ge(s_out, 16 * PAIRS)

        @block.gpsimd
        def _(pool):
            pool.memset(ident[:, :], 0.0).then_inc(pool_step, 1)
            pool.memset(centre[:, :], -1.0 / DIM).then_inc(pool_step, 1)
            pool.memset(nhalf[:, :], -0.5).then_inc(pool_step, 1)
            pool.memset(ones[:, :], 1.0).then_inc(pool_step, 1)
            pool.memset(epst[:, :], EPS).then_inc(pool_step, 1)
            pool.wait_ge(pool_step, 2)
            pool.affine_select(out=ident[:, :], in_=ident[:, :], compare_op=ALU.not_equal, fill=1.0, base=0,
                               pattern=[[-1, P]], channel_multiplier=1).then_inc(pool_step, 1)
            pool.affine_select(out=centre[:, :], in_=centre[:, :], compare_op=ALU.not_equal, fill=1.0 - 1.0 / DIM,
                               base=0, pattern=[[-1, DIM]], channel_multiplier=1).then_inc(pool_step, 1)
            pool.wait_ge(pool_step, 7)
            pool.affine_select(out=centre[:, :], in_=centre[:, :], compare_op=ALU.not_equal, fill=1.0 - 1.0 / DIM,
                               base=-DIM, pattern=[[-1, DIM]], channel_multiplier=1).then_inc(pool_step, 1)
            pool.wait_ge(pool_step, 8)
            pool.memset(lbp[:, :], 0.0).then_inc(pool_const, 1)
            pool.memset(w1st[DIM:P, :, :], 0.0).then_inc(pool_zero, 1)
            pool.wait_ge(pool_zero, 1)
            pool.wait_ge(polar_q, 1)
            pool.tensor_tensor(pol[:, 7, :], pol[:, 6, :], nhalf[:, 0:DEPTH], ALU.pow).then_inc(polar_inv, 1)

            def input_rstd(g):
                a, b = g * GT, (g + 1) * GT
                pool.wait_ge(x_stats, g + 1)
                pool.tensor_tensor(VX[:, a:b], MV[:, a:b, 1], epst[:, :], ALU.add).then_inc(x_ve, 1)
                pool.wait_ge(x_ve, g + 1)
                pool.tensor_tensor(RX[:, a:b], VX[:, a:b], nhalf[:, :], ALU.pow).then_inc(x_rstd, 1)

            def norm(u, summed, eps_added, done):
                g = u % GROUPS
                pool.wait_ge(summed, u + 1)
                pool.tensor_tensor(VE[:, g, :], SS[:, g, :], epst[:, :], ALU.add).then_inc(eps_added, 1)
                pool.wait_ge(eps_added, u + 1)
                pool.tensor_tensor(RS[:, g, :], VE[:, g, :], nhalf[:, :], ALU.pow).then_inc(done, 1)

            def add_b2(u):
                g, L = u % GROUPS, u // GROUPS
                pool.wait_ge(a1, u + 1)
                if u == 0:
                    pool.wait_ge(b2_done, 1)
                pool.tensor_tensor(by_tile(HB[:, g, :]), by_tile(H[:, g, :]),
                                   b2st[:, L, :].unsqueeze(1).to_broadcast([P, GT, DIM]), ALU.add).then_inc(hb, 1)

            def step(s):
                if s < GROUPS:
                    norm(s, ss1, ve1, rs1)
                if s + 1 < GROUPS:
                    input_rstd(s + 1)
                if 0 <= s - 1 < UNITS:
                    add_b2(s - 1)
                    norm(s - 1, ss2, ve2, rs2)
                if GROUPS <= s + 1 < STEPS:
                    norm(s + 1, ss1, ve1, rs1)

            def pair_rstd(k, done, src, mid, mid_done, dst, dst_done):
                a, b = 2 * k, 2 * k + 2
                pool.wait_ge(done, b)
                pool.tensor_tensor(mid[:, a:b], src[:, a:b], epst[:, 0:2], ALU.add).then_inc(mid_done, 1)
                pool.wait_ge(mid_done, k + 1)
                pool.tensor_tensor(dst[:, a:b], mid[:, a:b], nhalf[:, 0:2], ALU.pow).then_inc(dst_done, 1)

            pool.wait_ge(polar_inv, 1)
            pool.memset(Z2[DIM:P, :, :], 0.0).then_inc(pool_zero, 1)
            pool.wait_ge(pool_zero, 2)
            pool.memset(Z2[DIM:DIM + 1, :, :], 1.0).then_inc(pool_zero, 1)
            pool.wait_ge(pool_zero, 3)
            input_rstd(0)
            for s in range(STEPS - EARLY):
                step(s)
                if s == 3:
                    pool.wait_ge(rs1, s + 2)
                    pool.memset(WO[DIM:P, :], 0.0).then_inc(pool_zero, 1)
                    pool.wait_ge(pool_zero, 4)
                if s == 11:
                    pool.wait_ge(sums_ready, 2)
                    pool.wait_ge(late_read, 4)
                    pool.tensor_scalar(sm[:, 2:4], sm[:, 0:2], -1.0 / VOCAB, 0.0, ALU.mult, ALU.add) \
                        .then_inc(sums_scaled, 1)
            for k in range(PAIRS + 1):
                if k < EARLY:
                    step(STEPS - EARLY + k)
                if k >= 1:
                    pair_rstd(k - 1, mv1_done, MV1[:, :, 1], V1X, v1_ve, R1X, r1_ready)
                if k < PAIRS:
                    pair_rstd(k, o_sq, OSQ, OV, o_ve, OR, o_rstd)
            for k in range(PAIRS):
                pair_rstd(k, z_sq, ZQ, ZV, z_ve, ZR, z_rstd)
                for t in (2 * k, 2 * k + 1):
                    if t in POOL_TILES:
                        pool.wait_ge(z_rstd, k + 1)
                        pool.tensor_tensor(XN[:, t, :], XN[:, t, :], ZR[:, t:t + 1].to_broadcast([P, VOCAB]),
                                           ALU.mult).then_inc(pool_out, 1)
                        pool.wait_ge(pool_out, 2 * POOL_TILES.index(t) + 1)
                        pool.tensor_tensor(X[:, t, :], X[:, t, :], XN[:, t, :], ALU.add).then_inc(pool_out, 1)

        @block.scalar
        def _(act):
            act.wait_ge(pool_const, 1)
            act.wait_ge(s_ch, 16)
            for L in range(DEPTH):
                act.activation(cvst[:, L, MX0:MX0 + DIM], centre[:, :], ACT.Copy,
                               scale=chp[:, CH["scl"] + L:CH["scl"] + L + 1])
            act.activation(cvst[:, :, LW0], chc("w"), ACT.Copy)
            act.activation(cvst[:, :, LB0], chc("b"), ACT.Copy).then_inc(cv_store, 1)
            act.wait_ge(polar_r, 1)
            act.activation(pol[:, 9, :], pol[:, 8, :], ACT.Tanh).then_inc(decay, 1)
            act.wait_ge(decay, 1)
            for L in range(DEPTH):
                for q in range(SG):
                    lo = DC0 + q * SL + 1
                    last = act.activation(cvst[:, L, lo:lo + LEN], ones[:, :].unsqueeze(1).to_broadcast([P, 2, P]),
                                          ACT.Copy, scale=pol[:, 9, L:L + 1])
            last.then_inc(cv_store, 1)
            act.wait_ge(cv_store, 2)
            act.wait_ge(s_c64, 16)
            for L in range(DEPTH):
                act.activation(w1st[0:DIM, L, :], c6c("w1t", L * DFF, (L + 1) * DFF), ACT.Copy,
                               scale=c6c("w2", L, L + 1)).then_inc(w1_store, 1)
            act.activation(lbp[:, DIM:DIM + 1], c6c("lb"), ACT.Copy).then_inc(act_step, 1)

            def b1_out():
                act.wait_ge(b1_mm, 1)
                act.activation(sm[:, 8:16], LB[:, 0:8], ACT.Copy).then_inc(b1_read, 1)

            def setup_late(i):
                if i == 0:
                    act.activation(WOR[0:DIM, :], c6c("wout"), ACT.Copy, scale=c6c("lw"),
                                   accum_out=sm[0:DIM, 0:1]).then_inc(sums_ready, 1)
                    return
                act.wait_ge(late_mm, i + 1)
                if i == 1:
                    act.activation(rkT[:, :], LB[0:RDIM, 0:NSLOT], ACT.Copy).then_inc(late_read, 1)
                if i == 2:
                    act.activation(vpT[:, :], LB[0:VB, 0:NSLOT], ACT.Copy).then_inc(late_read, 1)
                if i == 3:
                    act.activation(KB[:, NSLOT:2 * NSLOT], c6c("keys"), ACT.Copy, scale=float(BOT) ** -0.5)
                    act.activation(KB[:, 0:NSLOT], LB[0:BOT, 0:NSLOT], ACT.Copy, scale=float(RDIM) ** -0.5) \
                        .then_inc(late_read, 1)
                if i == 4:
                    act.activation(V2R[:, :], LB[:, :], ACT.Copy, accum_out=sm[:, 1:2]).then_inc(late_read, 1)
                if i >= 5:
                    c = 2 * (i - 5)
                    act.activation(SW_[:, c:c + 2, 0:2 * NSLOT], LB[:, :].rearrange("p (c n) -> p c n", c=2),
                                   ACT.Copy).then_inc(late_read, 1)

            def setup_last():
                act.wait_ge(sums_scaled, 1)
                act.wait_ge(pool_zero, 4)
                act.activation(V2[:, :], V2R[:, :], ACT.Identity, bias=sm[:, 3:4])
                act.activation(WO[0:DIM + 1, :], WOR[:, :], ACT.Identity, bias=sm[0:DIM + 1, 2:3]).then_inc(late_ready, 1)

            def square(u, ready, done):
                g = u % GROUPS
                if ready is not None:
                    act.wait_ge(*ready)
                act.activation(SQ[:, g, :], H[:, g, :], ACT.Square, scale=float(DIM) ** -0.5).then_inc(done, 1)

            def silu1(u):
                g, L = u % GROUPS, u // GROUPS
                act.wait_ge(t1, u + 1)
                act.activation(by_seq(Y[:, g, :])[:, :, 1:SL], by_seq(T1B[:, :]), ACT.Silu,
                               bias=cvst[:, L, LB0:LB0 + 1], scale=cvst[:, L, LW0:LW0 + 1]).then_inc(y1, 1)

            def last_z(u):
                act.wait_ge(t1, u + 1)
                act.activation(Z2[0:DIM, u % GROUPS, :], T1B[0:DIM, :], ACT.Copy).then_inc(y1, 1)

            def z_out(u):
                act.wait_ge(t2, u + 1)
                act.activation(Z2[0:DIM, u % GROUPS, :], T2B[0:DIM, :], ACT.Copy).then_inc(e2, 1)

            def silu2(u, a):
                g, L = u % GROUPS, u // GROUPS
                act.wait_ge(f2, 2 * u + a + 1)
                if u == 0:
                    act.wait_ge(ff_done, 1)
                act.activation(HD[:, u % 2, a, :], FB[(2 * u + a) % 3][:, :], ACT.Silu,
                               bias=ffst[:, L, 2 * P + a:2 * P + a + 1]).then_inc(g2, 1)

            def step(s):
                if s < GROUPS:
                    square(s, (h0_done, s + 1), sq1)
                ffn = 0 <= s - 2 < UNITS
                if ffn:
                    z_out(s - 2)
                if 0 <= s - 1 < UNITS:
                    square(s - 1, (a1, s), sq2)
                if GROUPS <= s + 1 < STEPS:
                    square(s + 1, (a2, s - GROUPS + 2), sq1)
                if s < UNITS:
                    silu1(s)
                else:
                    last_z(s)
                if ffn:
                    silu2(s - 2, 0)
                    silu2(s - 2, 1)

            def out_square(t):
                act.wait_ge(o_mm, t + 1)
                if t >= 2:
                    act.wait_ge(o_sq, t - 1)
                act.activation(JK[:, t % 2, :], OB[t % 2][:, :], ACT.Square, scale=float(VOCAB) ** -0.5,
                               accum_out=OSQ[:, t:t + 1]).then_inc(o_sq, 1)

            def xn_out(t):
                act.wait_ge(xtr, t + 1)
                act.activation(XNT[:, t % 4, 0:GW], XB[t % 2][:, :], ACT.Copy).then_inc(xtr_read, 1)

            def gelu(t):
                act.wait_ge(s_mm, t + 1)
                if t >= 4:
                    act.wait_ge(lrn_done, t - 3)
                act.activation(GE[:, t % 4, :], SBK[t % 4][:, 2 * NSLOT:SW], ACT.Gelu_apprx_tanh) \
                    .then_inc(gelu_done, 1)

            for s in range(STEPS - EARLY):
                if s == 1:
                    b1_out()
                if s == LATE0 + LATES + 2:
                    setup_last()
                step(s)
                if 0 <= s - LATE0 < LATES:
                    setup_late(s - LATE0)
            def exps(k):
                act.wait_ge(am_max, k + 1)
                if k >= 2:
                    act.wait_ge(e_tr, k - 1)
                for j in range(2):
                    t = 2 * k + j
                    act.activation(E_[:, k % 2, j * NSLOT:(j + 1) * NSLOT], AM[:, t, :], ACT.Exp,
                                   bias=NMX[:, t:t + 1], accum_out=ES[:, t:t + 1]).then_inc(e_ready, 1)

            def e_out(k):
                act.wait_ge(e_tr, k + 1)
                act.activation(ET[:, k % 2, :], XB[k % 2][:, 0:2 * P], ACT.Copy).then_inc(et_ready, 1)

            def z_square(t):
                act.wait_ge(zz_ready, t + 1)
                if t >= 2:
                    act.wait_ge(z_sq, t - 1)
                act.activation(JK[:, t % 2, :], XN[:, t, :], ACT.Square, scale=float(VOCAB) ** -0.5,
                               accum_out=ZQ[:, t:t + 1]).then_inc(z_sq, 1)

            for k in range(PAIRS + LAG):
                if k < EARLY:
                    step(STEPS - EARLY + k)
                back = 2 * (k - LAG)
                if back >= 0:
                    xn_out(back)
                    xn_out(back + 1)
                if k == PAIRS + LAG - 1:
                    act.wait_ge(ln_in, 1)
                    act.activation(GA[:, 3, :], GA[:, 2, :], ACT.Ln).then_inc(ln_out, 1)
                    exps(0)
                    exps(1)
                for j in range(2):
                    if k < PAIRS:
                        out_square(2 * k + j)
                    if back >= 0:
                        gelu(back + j)

            e_out(0)
            e_out(1)
            act.wait_ge(sig_in, 1)
            act.activation(GA[:, 9, :], GA[:, 8, :], ACT.Exp, scale=-1.0).then_inc(sig_out, 1)
            act.wait_ge(gate_in, 1)
            act.activation(GA[:, 16, :], GA[:, 15, :], ACT.Exp, scale=-1.0).then_inc(gate_out, 1)
            exps(2)
            for k in range(2, PAIRS + 2):
                if k < PAIRS:
                    e_out(k)
                z_square(2 * (k - 2))
                if k + 1 < PAIRS:
                    exps(k + 1)
                z_square(2 * (k - 2) + 1)

        @block.vector
        def _(dve):
            chain = [0]

            def link(ins):
                chain[0] += 1
                ins.then_inc(dve_step, 1)
                dve.wait_ge(dve_step, chain[0])

            for q in range(SG):
                dve.memset(Y[:, :, q * SL], 1.0)
                dve.memset(cvst[:, :, DC0 + q * SL], 0.0)
            dve.memset(wcc[:, :, DIM:P], 0.0)
            dve.memset(cvst[:, :, MX0 + DIM:MX0 + P], 0.0)
            dve.memset(ffst[:, :, 0:2 * P].rearrange("p l (a d) -> p l a d", a=2)[:, :, :, DIM:P], 0.0)
            dve.memset(sm[DIM:P, 0:1], 0.0)
            link(dve.memset(pick[:, :], 0.0))
            for i in range(3):
                dve.memset(pick[32 * i:32 * i + 1, :], 1.0)
            dve.memset(table[0:DIM, :, 0], 1.0)
            dve.memset(table[DIM:P, :, 0], 0.0)
            dve.memset(T2[0:DIM, :, 0], 0.0)
            link(dve.memset(T2[DIM:P, :, 0], 1.0))
            dve.wait_ge(s_win, 32)
            dve.tensor_reduce(sm[:, 16:20], winr[:, :, :], AX.X, ALU.add)
            link(dve.tensor_reduce(sm[:, 20:21], binr[:, :], AX.X, ALU.add))
            dve.scalar_tensor_tensor(out=winc[:, :, :], in0=rows(sm[:, 16:20], VC, DIM), scalar=-1.0 / DIM,
                                     in1=winr[:, :, :], op0=ALU.mult, op1=ALU.add).then_inc(win_ready, 1)
            link(dve.tensor_scalar(sm[:, 21:22], sm[:, 20:21], -1.0 / DIM, None, ALU.mult))
            link(dve.tensor_scalar(binc[:, :], binr[:, :], sm[:, 21:22], None, ALU.add))
            dve.wait_ge(s_ch, 16)
            dve.tensor_scalar(pol[:, 0, :], chc("re"), -1.0, None, ALU.mult)
            link(dve.tensor_scalar(pol[:, 1, :], chc("im"), -1.0, None, ALU.mult))
            dve.tensor_tensor(pol[:, 2, :], pol[:, 0, :], chc("re"), ALU.max)
            link(dve.tensor_tensor(pol[:, 3, :], pol[:, 1, :], chc("im"), ALU.max))
            link(dve.tensor_tensor(pol[:, 4, :], pol[:, 2, :], pol[:, 3, :], ALU.max))
            link(dve.tensor_scalar(pol[:, 5, :], pol[:, 4, :], TINY, None, ALU.max))
            link(dve.reciprocal(pol[:, 10, :], pol[:, 5, :]))
            dve.tensor_tensor(pol[:, 0, :], chc("re"), pol[:, 10, :], ALU.mult)
            link(dve.tensor_tensor(pol[:, 1, :], chc("im"), pol[:, 10, :], ALU.mult))
            dve.tensor_tensor(pol[:, 2, :], pol[:, 0, :], pol[:, 0, :], ALU.mult)
            link(dve.tensor_tensor(pol[:, 3, :], pol[:, 1, :], pol[:, 1, :], ALU.mult))
            link(dve.tensor_tensor(pol[:, 11, :], pol[:, 2, :], pol[:, 3, :], ALU.add))
            dve.tensor_scalar(pol[:, 6, :], pol[:, 11, :], 1.0, None, ALU.max).then_inc(polar_q, 1)
            dve.wait_ge(win_mean, 1)
            dve.scalar_tensor_tensor(out=wcc[:, :, 0:DIM], in0=D1B[:, 0:DIM].unsqueeze(1).to_broadcast([P, VC, DIM]),
                                     scalar=-1.0 / VOCAB, in1=winc[:, :, :], op0=ALU.mult,
                                     op1=ALU.add).then_inc(win_done, 1)
            dve.wait_ge(polar_inv, 1)
            link(dve.tensor_tensor(CS[:, 0, 2, :], pol[:, 1, :], pol[:, 7, :], ALU.mult))
            dve.tensor_scalar(CS[:, 0, 1, :], CS[:, 0, 2, :], -1.0, None, ALU.mult)
            dve.tensor_tensor(pol[:, 2, :], pol[:, 0, :], pol[:, 7, :], ALU.mult)
            dve.tensor_tensor(pol[:, 10, :], pol[:, 11, :], pol[:, 7, :], ALU.mult)
            link(dve.tensor_scalar(pol[:, 3, :], pol[:, 11, :], 0.5, None, ALU.is_lt))
            dve.tensor_tensor(pol[:, 8, :], pol[:, 10, :], pol[:, 4, :], ALU.mult).then_inc(polar_r, 1)
            link(dve.tensor_tensor(CS[:, 0, 0, :], pol[:, 2, :], pol[:, 3, :], ALU.add))

            def table_level(k, a, b):
                n, d = 1 << k, b - a
                size = d * n * (2 if k < 7 else 1)
                A = tmpA[:, :, :].rearrange("p l n -> p (l n)")[:, 0:size]
                B = tmpB[:, :, :].rearrange("p l n -> p (l n)")[:, 0:size]
                if k < 7:
                    A, B = (t.rearrange("p (l a n) -> p l a n", l=d, a=2) for t in (A, B))
                    old = both[:, a:b, :, 0:n]
                    dve.tensor_tensor(A, old, CS[:, k, 0, a:b].unsqueeze(2).unsqueeze(3).to_broadcast([P, d, 2, n]),
                                      ALU.mult)
                    dve.tensor_tensor(B, old, CS[:, k, 1:3, a:b].rearrange("p a l -> p l a").unsqueeze(3)
                                      .to_broadcast([P, d, 2, n]), ALU.mult)
                    dve.tensor_tensor(CS[:, 8, 0:2, a:b], CS[:, k, 0:2, a:b], CS[:, k, 0:2, a:b], ALU.mult)
                    dve.scalar_tensor_tensor(out=CS[:, k + 1, 1:3, a:b], in0=CS[:, k, 1:3, a:b], scalar=2.0,
                                             in1=CS[:, k, 0, a:b].unsqueeze(1).to_broadcast([P, 2, d]), op0=ALU.mult,
                                             op1=ALU.mult).then_inc(dve_step, 1)
                    chain[0] += 1
                    dve.wait_ge(dve_step, chain[0])
                    dve.tensor_tensor(table[:, a:b, n:2 * n], A[:, :, 0, :], B[:, :, 1, :], ALU.add)
                    dve.tensor_tensor(T2[:, a:b, n:2 * n], A[:, :, 1, :], B[:, :, 0, :], ALU.add)
                    link(dve.tensor_tensor(CS[:, k + 1, 0, a:b], CS[:, 8, 0, a:b], CS[:, 8, 1, a:b], ALU.subtract))
                else:
                    A, B = (t.rearrange("p (l n) -> p l n", l=d) for t in (A, B))
                    dve.tensor_tensor(A, table[:, a:b, 0:n], rows(CS[:, k, 0, a:b], d, n), ALU.mult)
                    link(dve.tensor_tensor(B, T2[:, a:b, 0:n], rows(CS[:, k, 2, a:b], d, n), ALU.mult))
                    dve.tensor_tensor(table[:, a:b, n:2 * n], A, B, ALU.add).then_inc(table_done, 1)

            def first_state():
                dve.tensor_tensor(pol[:, 0, :], CS[:, 0, 0, :], chc("lre"), ALU.mult)
                dve.tensor_tensor(pol[:, 1, :], CS[:, 0, 1, :], chc("lim"), ALU.mult)
                dve.tensor_tensor(pol[:, 3, :], CS[:, 0, 2, :], chc("lre"), ALU.mult)
                link(dve.tensor_tensor(pol[:, 4, :], CS[:, 0, 0, :], chc("lim"), ALU.mult))
                dve.tensor_tensor(cvst[0:DIM, :, TA0], pol[0:DIM, 0, :], pol[0:DIM, 1, :], ALU.add)
                link(dve.tensor_tensor(pol[:, 2, :], pol[:, 3, :], pol[:, 4, :], ALU.add))
                dve.tensor_scalar(cvst[DIM:P, :, TA0], pol[DIM:P, 2, :], -1.0, None, ALU.mult).then_inc(state_done, 1)

            first_state()
            for k in range(8):
                table_level(k, 0, 1)

            def ffn_constants():
                dve.wait_ge(s_w2, 48)
                dve.tensor_reduce(sm[:, 24:32], w2r[:, :, :], AX.X, ALU.add)
                link(dve.tensor_reduce(sm[:, 32:32 + DEPTH], b2r[:, :, :], AX.X, ALU.add))
                dve.scalar_tensor_tensor(out=b2st[:, :, :], in0=rows(sm[:, 32:32 + DEPTH], DEPTH, DIM),
                                         scalar=-1.0 / DIM, in1=b2r[:, :, :], op0=ALU.mult,
                                         op1=ALU.add).then_inc(b2_done, 1)
                for L in range(DEPTH):
                    dve.scalar_tensor_tensor(out=ffst[:, L, 0:2 * P].rearrange("p (a d) -> p a d", a=2)[:, :, 0:DIM],
                                             in0=rows(sm[:, 24 + 2 * L:26 + 2 * L], 2, DIM), scalar=-1.0 / DIM,
                                             in1=w2r[:, 2 * L:2 * L + 2, :], op0=ALU.mult, op1=ALU.add)
                dve.wait_ge(b1_read, 1)
                dve.tensor_tensor(ffst[:, :, 2 * P:2 * P + 2], sm[:, 8:16].rearrange("p (l a) -> p l a", a=2),
                                  b1r[:, :].rearrange("p (l a) -> p l a", a=2), ALU.add).then_inc(ff_done, 1)

            def wo_bias():
                dve.wait_ge(late_mm, 1)
                dve.wait_ge(s_rows, 48)
                dve.tensor_tensor(WOR[DIM:DIM + 1, :], LB[DIM:DIM + 1, :], WOR[DIM:DIM + 1, :],
                                  ALU.add).then_inc(wo_row, 1)
                dve.wait_ge(wo_row, 1)
                dve.tensor_reduce(sm[DIM:DIM + 1, 0:1], WOR[DIM:DIM + 1, :], AX.X, ALU.add).then_inc(sums_ready, 1)

            def score_rows():
                dve.wait_ge(s_rows, 48)
                link(dve.tensor_copy(SWB[:, :], SWR[:, :]))
                link(dve.tensor_tensor(SWD[:, :], SWR[:, :], SWB[:, :], ALU.subtract))
                dve.tensor_copy(SWB[32:64, :], SWD[32:64, :])
                link(dve.tensor_copy(SWB[64:96, :], SWD[64:96, :]))
                link(dve.tensor_tensor(SWR[64:96, :], SWD[64:96, :], SWB[64:96, :], ALU.subtract))
                dve.tensor_copy(SWB[64:96, :], SWR[64:96, :]).then_inc(rows_done, 1)

            def input_stats(g):
                dve.wait_ge(s_x[g], 16)
                for t in range(g * GT, (g + 1) * GT):
                    dve.bn_stats(BN[:, t, :], X[:, t, :]).then_inc(bn_done, 1)
                for t in range(g * GT, (g + 1) * GT):
                    dve.wait_ge(bn_done, t + 1)
                    last = dve.bn_aggr(MV[:, t, :], BN[:, t, :])
                last.then_inc(x_stats, 1)

            def first_h(g):
                dve.wait_ge(h0_mm, g + 1)
                dve.wait_ge(x_rstd, g + 1)
                for j in range(GT):
                    t = g * GT + j
                    last = dve.scalar_tensor_tensor(out=H[:, g, j * DIM:(j + 1) * DIM],
                                                    in0=HB0[g][:, j * P:j * P + DIM], scalar=RX[:, t:t + 1],
                                                    in1=binc[:, :], op0=ALU.mult, op1=ALU.add)
                last.then_inc(h0_done, 1)

            def sum_squares(u, squared, done):
                g = u % GROUPS
                dve.wait_ge(squared, u + 1)
                dve.tensor_reduce(SS[:, g, :], by_tile(SQ[:, g, :]), AX.X, ALU.add).then_inc(done, 1)

            def scale_twice(u):
                g = u % GROUPS
                dve.wait_ge(rs1, u + 1)
                dve.tensor_tensor(Z[:, g, :].rearrange("p (j a d) -> p j a d", j=GT, a=2),
                                  by_tile(H[:, g, :]).unsqueeze(2).to_broadcast([P, GT, 2, DIM]),
                                  RS[:, g, :].unsqueeze(2).unsqueeze(3).to_broadcast([P, GT, 2, DIM]),
                                  ALU.mult).then_inc(z1, 1)

            def scale(u, ready, done):
                g = u % GROUPS
                dve.wait_ge(ready, u + 1)
                dve.tensor_tensor(by_tile(Z[:, g, 0:HC]), by_tile(H[:, g, :]), rows(RS[:, g, :], GT, DIM),
                                  ALU.mult).then_inc(done, 1)

            def modulate(u):
                g, L = u % GROUPS, u // GROUPS
                dve.wait_ge(y1, u + 1)
                if u == 0:
                    dve.wait_ge(table_done, 1)
                    dve.wait_ge(state_done, 1)
                if u == GROUPS:
                    dve.wait_ge(table_done, 2)
                dve.tensor_tensor(by_seq(U[:, g, :]), by_seq(Y[:, g, :]),
                                  cvst[:, L, TA0:TA0 + SL].unsqueeze(1).to_broadcast([P, SG, SL]),
                                  ALU.mult).then_inc(u1, 1)

            def scan(u):
                g, L = u % GROUPS, u // GROUPS
                dve.wait_ge(u1, u + 1)
                if u == 0:
                    dve.wait_ge(cv_store, 2)
                dve.tensor_tensor_scan(V[:, g, :], cvst[:, L, DC0:DC0 + UC], U[:, g, :], 0.0, ALU.mult,
                                       ALU.add).then_inc(v1, 1)

            def demodulate(u):
                g, L = u % GROUPS, u // GROUPS
                dve.wait_ge(v1, u + 1)
                dve.tensor_tensor(by_seq(U[:, g, 0:GW]), by_seq(V[:, g, :])[:, :, 1:SL],
                                  cvst[:, L, TA0 + 1:TA0 + SL].unsqueeze(1).to_broadcast([P, SG, LEN]),
                                  ALU.mult).then_inc(w1, 1)

            def add_conv(u):
                g = u % GROUPS
                dve.wait_ge(d1, u + 1)
                dve.tensor_tensor(by_tile(H[:, g, :]), by_tile(D1B[:, :])[:, :, 0:DIM], by_tile(H[:, g, :]),
                                  ALU.add).then_inc(a1, 1)

            def add_ffn(u):
                g = u % GROUPS
                dve.wait_ge(d2, u + 1)
                dve.wait_ge(hb, u + 1)
                dve.tensor_tensor(by_tile(H[:, g, :]), by_tile(D2B[:, :])[:, :, 0:DIM], by_tile(HB[:, g, :]),
                                  ALU.add).then_inc(a2, 1)

            def step(s):
                conv = 0 <= s - 1 < UNITS
                if conv:
                    scan(s - 1)
                if s < GROUPS:
                    sum_squares(s, sq1, ss1)
                if 0 <= s - 2 < UNITS:
                    scale(s - 2, rs2, z2)
                if conv:
                    demodulate(s - 1)
                if 0 <= s - 3 < UNITS:
                    add_ffn(s - 3)
                if s + 1 < GROUPS:
                    input_stats(s + 1)
                if s < UNITS:
                    scale_twice(s)
                else:
                    scale(s, rs1, z1)
                if s == 1:
                    ffn_constants()
                for k in {0: (0, 1, 2, 3), 2: (4, 5), 3: (6, 7)}.get(s, ()):
                    table_level(k, 1, DEPTH)
                if conv:
                    add_conv(s - 1)
                    sum_squares(s - 1, sq2, ss2)
                if GROUPS <= s + 1 < STEPS:
                    sum_squares(s + 1, sq1, ss1)
                if s == LATE0:
                    wo_bias()
                if s == LATE0 + 2:
                    score_rows()
                if s + 1 < GROUPS:
                    first_h(s + 1)
                if s < UNITS:
                    modulate(s)

            def first_result(t):
                dve.wait_ge(o_rstd, t // 2 + 1)
                dve.scalar_tensor_tensor(out=X[:, t, :], in0=OB[t % 2][:, :], scalar=OR[:, t:t + 1],
                                         in1=X[:, t, :], op0=ALU.mult, op1=ALU.add).then_inc(x1_done, 1)

            def first_stats(t):
                dve.wait_ge(x1_done, t + 1)
                dve.bn_stats(BN[:, t, :], X[:, t, :]).then_inc(bn1_done, 1)

            def first_mean(t):
                dve.wait_ge(bn1_done, t + 1)
                dve.bn_aggr(MV1[:, t, :], BN[:, t, :]).then_inc(mv1_done, 1)

            def normalise(t):
                dve.wait_ge(r1_ready, t // 2 + 1)
                dve.tensor_scalar(XN[:, t, :], X[:, t, :], MV1[:, t, 0:1], R1X[:, t:t + 1], ALU.subtract,
                                  ALU.mult).then_inc(xn_done, 1)

            def learned(t):
                dve.scalar_tensor_tensor(out=GJ[:, t % 2, :], in0=GE[:, t % 4, :], scalar=1.0, in1=ltc("wu2"),
                                         op0=ALU.mult, op1=ALU.mult, accum_out=LRN[:, t:t + 1]).then_inc(lrn_done, 1)

            def select_pair(t0):
                for t in (t0, t0 + 1):
                    dve.wait_ge(gelu_done, t + 1)
                    dve.max(M8[:, t % 2, :], SBK[t % 4][:, 0:NSLOT]).then_inc(top_found, 1)
                learned(t0)
                learned(t0 + 1)
                if t0 + 2 == TILES:
                    gate_learned()
                for t in (t0, t0 + 1):
                    dve.wait_ge(top_found, t + 1)
                    dve.match_replace(REP[:, t % 4, :], M8[:, t % 2, :], SBK[t % 4][:, 0:NSLOT],
                                      LOWEST).then_inc(top_marked, 1)
                q = t0 % 4
                dve.wait_ge(top_marked, t0 + 2)
                dve.tensor_scalar(OFS[:, q:q + 2, :], REP[:, q:q + 2, :], LOWEST, -BIG, ALU.not_equal,
                                  ALU.mult).then_inc(top_ofs, 1)
                dve.wait_ge(top_ofs, t0 // 2 + 1)
                for t in (t0, t0 + 1):
                    dve.tensor_tensor(AM[:, t, :], SBK[t % 4][:, NSLOT:2 * NSLOT], OFS[:, t % 4, :],
                                      ALU.add).then_inc(sc_read, 1)

            def pair_max(k):
                dve.wait_ge(sc_read, 2 * k + 2)
                dve.tensor_reduce(NMX[:, 2 * k:2 * k + 2], AM[:, 2 * k:2 * k + 2, :], AX.X, ALU.max,
                                  negate=True).then_inc(am_max, 1)

            input_stats(0)
            first_h(0)
            for s in range(STEPS - EARLY):
                step(s)
            steps = [0]

            def gstep(ins):
                steps[0] += 1
                ins.then_inc(ga_step, 1)
                dve.wait_ge(ga_step, steps[0])

            def gate_variance():
                dve.wait_ge(r1_ready, PAIRS)
                gstep(dve.tensor_tensor(GA[:, 0, :], R1X[:, :], R1X[:, :], ALU.mult))
                gstep(dve.tensor_tensor(GA[:, 1, :], GA[:, 0, :], MV1[:, :, 1], ALU.mult))
                dve.tensor_scalar(GA[:, 2, :], GA[:, 1, :], 1.0, None, ALU.add).then_inc(ln_in, 1)
                dve.wait_ge(ln_in, 1)
                gstep(dve.tensor_scalar(GA[:, 4, :], GA[:, 2, :], 1.0, None, ALU.subtract))
                gstep(dve.tensor_scalar(GA[:, 5, :], GA[:, 4, :], 0.0, None, ALU.is_equal))
                gstep(dve.tensor_tensor(GA[:, 6, :], GA[:, 4, :], GA[:, 5, :], ALU.add))
                dve.tensor_tensor(GA[:, 11, :], GA[:, 5, :], GA[:, 1, :], ALU.mult)
                gstep(dve.reciprocal(GA[:, 7, :], GA[:, 6, :]))
                gstep(dve.tensor_tensor(GA[:, 10, :], GA[:, 7, :], GA[:, 1, :], ALU.mult))

            def gate_sum():
                dve.wait_ge(ln_out, 1)
                gstep(dve.tensor_tensor(GA[:, 12, :], GA[:, 3, :], GA[:, 10, :], ALU.mult))
                gstep(dve.tensor_tensor(GA[:, 13, :], GA[:, 12, :], GA[:, 11, :], ALU.add))
                dve.tensor_reduce(gsum[:, 0:1], GA[:, 13, :], AX.X, ALU.add).then_inc(gsum_in, 1)

            def gate_learned():
                dve.wait_ge(lrn_done, TILES)
                dve.tensor_scalar(GA[:, 8, :], LRN[:, :], ltc("bu2"), -80.0, ALU.add, ALU.max).then_inc(sig_in, 1)

            def gate_mean():
                dve.wait_ge(gsum_mm, 1)
                dve.tensor_scalar(gsum[:, 1:2], OB[0][:, 0:1], 1.0 / TOK, 1e-6, ALU.mult, ALU.add) \
                    .then_inc(gsum_read, 1)
                dve.wait_ge(gsum_read, 1)
                gstep(dve.reciprocal(gsum[:, 2:3], gsum[:, 1:2]))
                gstep(dve.tensor_scalar(GA[:, 14, :], GA[:, 13, :], gsum[:, 2:3], 0.5, ALU.mult, ALU.mult))

            def gate():
                dve.wait_ge(sig_out, 1)
                gstep(dve.tensor_scalar(GA[:, 17, :], GA[:, 9, :], 1.0, None, ALU.add))
                gstep(dve.reciprocal(GA[:, 18, :], GA[:, 17, :]))
                gstep(dve.scalar_tensor_tensor(out=GA[:, 19, :], in0=GA[:, 18, :], scalar=2.5, in1=GA[:, 14, :],
                                               op0=ALU.mult, op1=ALU.add))
                gstep(dve.tensor_scalar(GA[:, 20, :], GA[:, 19, :], 0.0, 5.0, ALU.max, ALU.min))
                gstep(dve.tensor_scalar(GA[:, 21, :], GA[:, 20, :], 0.5, 1.0 / 1.5, ALU.subtract, ALU.mult))
                gstep(dve.tensor_scalar(GA[:, 22, :], GA[:, 21, :], 0.0, 1.0, ALU.max, ALU.min))
                gstep(dve.tensor_scalar(GA[:, 23, :], GA[:, 22, :], ltc("gw"), ltc("gb"), ALU.mult, ALU.add))
                dve.tensor_scalar(GA[:, 15, :], GA[:, 23, :], -80.0, None, ALU.max).then_inc(gate_in, 1)
                dve.wait_ge(gate_out, 1)
                gstep(dve.tensor_scalar(GA[:, 0, :], GA[:, 16, :], 1.0, None, ALU.add))
                gstep(dve.reciprocal(GA[:, 1, :], GA[:, 0, :]))
                gstep(dve.scalar_tensor_tensor(out=GA[:, 4, :], in0=GA[:, 1, :], scalar=0.05, in1=GA[:, 1, :],
                                               op0=ALU.is_ge, op1=ALU.mult))

            def first(p):
                for t in (2 * p, 2 * p + 1):
                    first_result(t)
                for t in (2 * p, 2 * p + 1):
                    first_stats(t)
                for t in (2 * p, 2 * p + 1):
                    first_mean(t)

            for k in range(PAIRS + LAG + 1):
                if k < EARLY:
                    step(STEPS - EARLY + k)
                back = 2 * (k - LAG - 1)
                if 0 <= k - 1 < PAIRS:
                    first(k - 1)
                if k == PAIRS + LAG - 1:
                    gate_sum()
                if k == PAIRS + LAG:
                    gate_mean()
                if back >= 0:
                    select_pair(back)
                    pair_max(back // 2)
                if 0 <= k - 1 < PAIRS:
                    normalise(2 * k - 2)
                    normalise(2 * k - 1)
                if k == PAIRS:
                    gate_variance()
            gate()

            def invert(k):
                dve.wait_ge(e_ready, 2 * k + 2)
                dve.reciprocal(RES[:, 2 * k:2 * k + 2], ES[:, 2 * k:2 * k + 2]).then_inc(es_inv, 1)

            def weigh(k):
                a, b = 2 * k, 2 * k + 2
                dve.wait_ge(es_inv, k + 1)
                dve.tensor_tensor(GS[:, a:b], RES[:, a:b], GA[:, 4, a:b], ALU.mult).then_inc(gs_ready, 1)

            def mix(t):
                dve.wait_ge(gs_ready, t // 2 + 1)
                dve.wait_ge(aux_mm, t + 1)
                dve.scalar_tensor_tensor(out=XN[:, t, :], in0=MB[t % 4][:, :], scalar=GS[:, t:t + 1],
                                         in1=XN[:, t, :], op0=ALU.mult, op1=ALU.add).then_inc(zz_ready, 1)

            def finish(t):
                dve.wait_ge(z_rstd, t // 2 + 1)
                dve.scalar_tensor_tensor(out=X[:, t, :], in0=XN[:, t, :], scalar=ZR[:, t:t + 1],
                                         in1=X[:, t, :], op0=ALU.mult, op1=ALU.add).then_inc(out_ready, 1)

            invert(0)
            for k in range(PAIRS + 2):
                if k < PAIRS:
                    weigh(k)
                    mix(2 * k)
                    mix(2 * k + 1)
                if k + 1 < PAIRS:
                    invert(k + 1)
                if k >= 2:
                    for t in (2 * k - 4, 2 * k - 3):
                        if t not in POOL_TILES:
                            finish(t)

        @block.tensor
        def _(pe):
            pe.wait_ge(pool_const, 1)
            pe.wait_ge(win_ready, 1)
            for c in range(VC):
                last = pe.matmul(D1B[:, 0:DIM], ones[:, :], winc[:, c, :], start=(c == 0), stop=(c == VC - 1))
            last.then_inc(win_mean, 1)

            def setup_ffn():
                pe.wait_ge(s_c64, 16)
                for k in range(2 * DEPTH):
                    last = pe.matmul(LB[:, k:k + 1], c6c("w1t", k * P, (k + 1) * P),
                                     c6c("b2", k // 2, k // 2 + 1), start=True, stop=True)
                last.then_inc(b1_mm, 1)

            def setup_late(i):
                if i == 0:
                    pe.wait_ge(act_step, 1)
                    pe.wait_ge(h0_done, GROUPS)
                    last = pe.matmul(LB[0:DIM + 1, :], lbp[:, :], c6c("wout"), start=True, stop=True)
                if i == 1:
                    pe.wait_ge(wo_row, 1)
                    last = pe.matmul(LB[0:RDIM, 0:NSLOT], c6c("wrt"), c6c("keys"), start=True, stop=True)
                if i >= 2:
                    pe.wait_ge(late_read, i - 1)
                if i == 2:
                    pe.wait_ge(s_late, 48)
                    vals = ltc("vals").rearrange("p (c n) -> p c n", c=VC)
                    wvd = ltc("wvd").rearrange("p (c n) -> p c n", c=VC)
                    for c in range(VC):
                        last = pe.matmul(LB[0:VB, 0:NSLOT], wvd[:, c, :], vals[:, c, :], start=(c == 0),
                                         stop=(c == VC - 1))
                if i == 3:
                    last = pe.matmul(LB[0:BOT, 0:NSLOT], wr_s[:, :], rkT[:, :], start=True, stop=True)
                if i == 4:
                    last = pe.matmul(LB[:, :], vpT[:, :], wvu_s[:, :], start=True, stop=True)
                if i >= 5:
                    for c in range(2 * (i - 5), 2 * (i - 5) + 2):
                        last = pe.matmul(LB[:, (c % 2) * 2 * NSLOT:(c % 2 + 1) * 2 * NSLOT],
                                         c6c("wq", c * P, (c + 1) * P), KB[:, :], start=True, stop=True)
                last.then_inc(late_mm, 1)

            def first_h(g):
                pe.wait_ge(s_xt[g], 16)
                if g == 0:
                    pe.wait_ge(win_done, 1)
                if g == 3:
                    pe.wait_ge(b1_read, 1)
                for j in range(GT):
                    for c in range(VC):
                        last = pe.matmul(HB0[g][:, j * P:(j + 1) * P], XT[:, g, c, j * P:(j + 1) * P],
                                         wcc[:, c, :], start=(c == 0), stop=(c == VC - 1))
                last.then_inc(h0_mm, 1)

            def turn1(u):
                g = u % GROUPS
                pe.wait_ge(z1, u + 1)
                if u >= 1:
                    pe.wait_ge(y1, u)
                for j in range(GT):
                    if u < UNITS:
                        last = pe.transpose(T1B[:, j * P:(j + 1) * P], Z[:, g, j * P:(j + 1) * P], ident[:, :])
                    else:
                        last = pe.transpose(T1B[0:DIM, j * P:(j + 1) * P], Z[:, g, j * DIM:(j + 1) * DIM],
                                            ident[:, :])
                last.then_inc(t1, 1)

            def mix_in(u):
                g, L = u % GROUPS, u // GROUPS
                pe.wait_ge(w1, u + 1)
                if u == 0:
                    pe.wait_ge(cv_store, 1)
                else:
                    pe.wait_ge(a1, u)
                for j in range(GT):
                    last = pe.matmul(D1B[:, j * P:(j + 1) * P], U[:, g, j * P:(j + 1) * P],
                                     cvst[:, L, MX0:MX0 + P], start=True, stop=True)
                last.then_inc(d1, 1)

            def turn2(u):
                g = u % GROUPS
                pe.wait_ge(z2, u + 1)
                if u >= 1:
                    pe.wait_ge(e2, u)
                for j in range(GT):
                    last = pe.transpose(T2B[0:DIM, j * P:(j + 1) * P], Z[:, g, j * DIM:(j + 1) * DIM], ident[:, :])
                last.then_inc(t2, 1)

            def hidden(u, a):
                g, L = u % GROUPS, u // GROUPS
                pe.wait_ge(e2, u + 1)
                if a == 0 and g == 0:
                    pe.wait_ge(w1_store, L + 1)
                if u == 0 and a == 0:
                    pe.wait_ge(pool_zero, 3)
                if 2 * u + a < 3:
                    pe.wait_ge(h0_done, 2 * u + a + 1)
                else:
                    pe.wait_ge(g2, 2 * u + a - 2)
                pe.matmul(FB[(2 * u + a) % 3][:, :], w1st[:, L, a * P:(a + 1) * P], Z2[:, g, :], start=True,
                          stop=True).then_inc(f2, 1)

            def project(u):
                g, L = u % GROUPS, u // GROUPS
                pe.wait_ge(g2, 2 * u + 2)
                if u >= 1:
                    pe.wait_ge(a2, u)
                for j in range(GT):
                    for a in range(2):
                        last = pe.matmul(D2B[:, j * P:(j + 1) * P], HD[:, u % 2, a, j * P:(j + 1) * P],
                                         ffst[:, L, a * P:(a + 1) * P], start=(a == 0), stop=(a == 1))
                last.then_inc(d2, 1)

            def step(s):
                if 0 <= s - 3 < UNITS:
                    project(s - 3)
                ffn = 0 <= s - 2 < UNITS
                if ffn:
                    turn2(s - 2)
                if 0 <= s - 1 < UNITS:
                    mix_in(s - 1)
                turn1(s)
                if ffn:
                    hidden(s - 2, 0)
                if s + 2 < GROUPS:
                    first_h(s + 2)
                if ffn:
                    hidden(s - 2, 1)

            def output(t):
                if t == 0:
                    pe.wait_ge(late_ready, 1)
                    pe.wait_ge(late_read, LATES - 1)
                    pe.wait_ge(a1, UNITS)
                pe.wait_ge(y1, UNITS + t // GT + 1)
                if t >= 2:
                    pe.wait_ge(x1_done, t - 1)
                pe.matmul(OB[t % 2][:, :], Z2[:, t // GT, (t % GT) * P:(t % GT + 1) * P], WO[:, :], start=True,
                          stop=True).then_inc(o_mm, 1)

            def turn_xn(t):
                pe.wait_ge(xn_done, t + 1)
                if t >= 2:
                    pe.wait_ge(xtr_read, t - 1)
                else:
                    pe.wait_ge(y1, STEPS)
                    pe.wait_ge(e2, UNITS)
                for c in range(VC):
                    last = pe.transpose(XB[t % 2][:, c * P:(c + 1) * P], XN[:, t, c * P:(c + 1) * P], ident[:, :])
                last.then_inc(xtr, 1)

            def scores(t):
                pe.wait_ge(xtr_read, t + 1)
                if t >= 4:
                    pe.wait_ge(sc_read, t - 3)
                else:
                    pe.wait_ge(g2, 2 * UNITS)
                    pe.wait_ge(a2, UNITS)
                    pe.wait_ge(rows_done, 1)
                pe.matmul(SBK[t % 4][:, 0:SW], pick[:, :], SWB[:, :], start=True, stop=False)
                for c in range(VC):
                    last = pe.matmul(SBK[t % 4][:, 0:SW], XNT[:, t % 4, c * P:(c + 1) * P], SW_[:, c, :],
                                     start=False, stop=(c == VC - 1))
                last.then_inc(s_mm, 1)

            first_h(0)
            first_h(1)
            setup_ffn()
            for s in range(STEPS - EARLY):
                step(s)
                if 0 <= s - LATE0 < LATES:
                    setup_late(s - LATE0)
            for k in range(PAIRS + LAG):
                if k < EARLY:
                    step(STEPS - EARLY + k)
                back = 2 * (k - LAG)
                if back >= 0:
                    turn_xn(back)
                    turn_xn(back + 1)
                for j in range(2):
                    if k < PAIRS:
                        output(2 * k + j)
                    if back >= 0:
                        scores(back + j)
                    if back + j == TILES - 2:
                        pe.wait_ge(gsum_in, 1)
                        pe.wait_ge(x1_done, TILES)
                        pe.matmul(OB[0][:, 0:1], ones[:, :], gsum[:, 0:1], start=True, stop=True).then_inc(gsum_mm, 1)
            def turn_e(k):
                pe.wait_ge(e_ready, 2 * k + 2)
                if k >= 2:
                    pe.wait_ge(et_ready, k - 1)
                for j in range(2):
                    last = pe.transpose(XB[k % 2][:, j * P:(j + 1) * P], E_[:, k % 2, j * P:(j + 1) * P],
                                        ident[:, :])
                last.then_inc(e_tr, 1)

            def memory(t):
                pe.wait_ge(et_ready, t // 2 + 1)
                if t >= 4:
                    pe.wait_ge(zz_ready, t - 3)
                elif t >= 2:
                    pe.wait_ge(sc_read, TILES - 2)
                else:
                    pe.wait_ge(gsum_read, 1)
                pe.matmul(MB[t % 4][:, :], ET[:, t // 2 % 2, (t % 2) * P:(t % 2 + 1) * P], V2[:, :], start=True,
                          stop=True).then_inc(aux_mm, 1)

            for k in range(PAIRS + 1):
                if k < PAIRS:
                    turn_e(k)
                if k >= 1:
                    memory(2 * k - 2)
                    memory(2 * k - 1)


def kernel(**inputs):
    import concourse.bacc as bacc
    from concourse import mybir as _mybir
    from concourse.bass_utils import run_bass_kernel_spmd

    a = {k.split("_", 2)[2] if k.startswith("L0_attn_") else k[7:]: np.asarray(v) for k, v in inputs.items()}

    def chunks(w):
        return w.T.reshape(VC, P, w.shape[0]).transpose(1, 0, 2)

    def twice(v):
        return np.concatenate([v.T, v.T], axis=0)

    def column(v):
        return np.broadcast_to(v.reshape(1, 1), (P, 1))

    x = a["x"].reshape(TOK, VOCAB)
    xT = x.reshape(GROUPS, GW, VC, P).transpose(3, 0, 2, 1)
    late = [chunks(a["aux_values"]), chunks(a["Wvd"]), np.broadcast_to(a["Wu2"], (P, UH)), column(a["bu2"]), column(a["gate_w1"]), column(a["gate_bias"])]
    c64 = [a["ln2_w"].T, a["ln2_b"].T, a["lnl_w"].reshape(DIM, 1), a["lnl_b"].reshape(DIM, 1),
           a["W1"].transpose(2, 0, 1).reshape(DIM, DEPTH * DFF), a["Wout"].T, a["Wr"].T, a["aux_keys"].T,
           a["Wq"]]
    arrays = {
        "x": x, "xT": xT, "win": chunks(a["Win"]),
        "binb": np.broadcast_to(a["bin"], (P, DIM)),
        "ch": np.concatenate([twice(a[n]) for n in ("phz_re", "phz_im", "lc_re", "lc_im", "sc_lin", "ln1_w", "ln1_b")],
                             axis=1),
        "c64": np.concatenate(c64, axis=1),
        "w2t": a["W2"].reshape(DEPTH, DIM, 2, P).transpose(3, 0, 2, 1).reshape(P, 2 * DEPTH, DIM),
        "b1": a["b1"].reshape(DEPTH * 2, P).T,
        "b2b": np.broadcast_to(a["b2"], (P, DEPTH, DIM)),
        "late": np.concatenate([v.reshape(P, -1) for v in late], axis=1),
        "wu1": chunks(a["Wu1"]), "wr": a["Wr"], "wvu": a["Wvu"].T, "boutr": a["bout"].reshape(1, VOCAB), 
        "srow": np.broadcast_to(np.concatenate([a["log_rel"], a["log_rel"], a["bu1"]]), (ROWS, SW)),
    }
    arrays = {k: np.ascontiguousarray(v) for k, v in arrays.items()}
    nc = bacc.Bacc("TRN2", target_bir_lowering=False, num_devices=1)
    args = [nc.dram_tensor(f"in_{k}", v.shape, _mybir.dt.from_np(v.dtype), kind="ExternalInput").ap()
            for k, v in arrays.items()]
    args.append(nc.dram_tensor("out_0", (TOK, VOCAB), _mybir.dt.float32, kind="ExternalOutput").ap())
    build(nc, *args)
    r = run_bass_kernel_spmd(nc, [{f"in_{k}": v for k, v in arrays.items()}], core_ids=[0])
    return r.results[0]["out_0"].reshape(SEQS, LEN, VOCAB)
```
